# Optimizing a Trainium2 kernel written in Bass

```python
import numpy as np
import jax
import jax.numpy as jnp

def _softmax(x, axis=-1):
    return jax.nn.softmax(x, axis=axis)

def _gelu(x):
    return jax.nn.gelu(x, approximate=True)

def _silu(x):
    return jax.nn.silu(x)

def _sigmoid(x):
    return jax.nn.sigmoid(x)

def _layernorm(x, axis=-1, eps=1e-05):
    m = jnp.mean(x, axis=axis, keepdims=True)
    v = jnp.var(x, axis=axis, keepdims=True)
    return (x - m) / jnp.sqrt(v + eps)

def _scatter_add(tgt, idx, src, axis=0):
    return tgt.at[idx].add(src)

def _segment_sum(src, seg, n):
    return jax.ops.segment_sum(src, seg, n)
kernel_name = 'mk_adj_resnorm_d2_adj_r2_5eb4c7'

def setup_inputs(seed: int=0):
    np.random.seed(seed)
    _w = jnp.asarray

    def _rec_inputs():
        import jax
        import jax.numpy as jnp
        _gk = jax.random.key(seed)
        x = -0.0002928 + 1 * jax.random.normal(jax.random.fold_in(_gk, 1), (8, 1024, 256), jnp.float32)
        _a = jax.random.bernoulli(jax.random.fold_in(_gk, 2), 0.015625, (1024, 1024))
        adj = _a.astype(jnp.int32)
        return (x, adj)
    x, adj = _rec_inputs()

    def _L0_gnn_setup():
        import jax, jax.numpy as jnp
        import numpy as np
        D_MODEL = 256
        NUM_HEADS = 8
        D_HEAD = D_MODEL // NUM_HEADS
        B, N = (4, 1024)
        key = jax.random.key(seed)
        ks = jax.random.split(key, 10)
        s = 1.0 / np.sqrt(D_MODEL)
        inp = {'h': jax.random.normal(ks[0], (B, N, D_MODEL), dtype=jnp.float32), 'adj': jax.random.randint(ks[1], (N, N), 0, 2, dtype=jnp.int32), 'Wq': jax.random.uniform(ks[2], (D_MODEL, D_MODEL), jnp.float32, -s, s), 'bq': jax.random.uniform(ks[3], (D_MODEL,), jnp.float32, -s, s), 'Wk': jax.random.uniform(ks[4], (D_MODEL, D_MODEL), jnp.float32, -s, s), 'bk': jax.random.uniform(ks[5], (D_MODEL,), jnp.float32, -s, s), 'Wv': jax.random.uniform(ks[6], (D_MODEL, D_MODEL), jnp.float32, -s, s), 'bv': jax.random.uniform(ks[7], (D_MODEL,), jnp.float32, -s, s), 'Wo': jax.random.uniform(ks[8], (D_MODEL, D_MODEL), jnp.float32, -s, s), 'bo': jax.random.uniform(ks[9], (D_MODEL,), jnp.float32, -s, s)}
        return inp
    _L0_gnn_all = _L0_gnn_setup()
    _L0_gnn_in = {k: v for k, v in _L0_gnn_all.items() if k in ('Wq', 'bq', 'Wk', 'bk', 'Wv', 'bv', 'Wo', 'bo')}
    del _L0_gnn_all

    def _L1_gnn_setup():
        import jax, jax.numpy as jnp
        import numpy as np
        B, K, DIN, DOUT = (32, 64, 256, 256)
        key = jax.random.key(seed)
        k1, k2, k3, k4 = jax.random.split(key, 4)
        x = jax.random.normal(k1, (B, K, DIN), dtype=jnp.float32)
        adj = jax.random.randint(k2, (K, K), 0, 2, dtype=jnp.int32)
        W = jax.random.normal(k3, (DOUT, 2 * DIN), dtype=jnp.float32) * 0.02
        b = jax.random.normal(k4, (DOUT,), dtype=jnp.float32) * 0.02
        return {'x': x, 'adj': adj, 'W': W, 'b': b}
    _L1_gnn_all = _L1_gnn_setup()
    _L1_gnn_in = {k: v for k, v in _L1_gnn_all.items() if k in ('W', 'b')}
    del _L1_gnn_all
    return {'x': x, 'adj': adj, 'L0_gnn_Wq': _L0_gnn_in['Wq'], 'L0_gnn_bq': _L0_gnn_in['bq'], 'L0_gnn_Wk': _L0_gnn_in['Wk'], 'L0_gnn_bk': _L0_gnn_in['bk'], 'L0_gnn_Wv': _L0_gnn_in['Wv'], 'L0_gnn_bv': _L0_gnn_in['bv'], 'L0_gnn_Wo': _L0_gnn_in['Wo'], 'L0_gnn_bo': _L0_gnn_in['bo'], 'L1_gnn_W': _L1_gnn_in['W'], 'L1_gnn_b': _L1_gnn_in['b']}

def reference(x, adj, L0_gnn_Wq, L0_gnn_bq, L0_gnn_Wk, L0_gnn_bk, L0_gnn_Wv, L0_gnn_bv, L0_gnn_Wo, L0_gnn_bo, L1_gnn_W, L1_gnn_b):
    import jax
    import jax.numpy as jnp

    def _L0_gnn_ref(h, adj, Wq, bq, Wk, bk, Wv, bv, Wo, bo):
        import jax, jax.numpy as jnp
        import numpy as np
        D_MODEL = 256
        NUM_HEADS = 8
        D_HEAD = D_MODEL // NUM_HEADS
        B, N = (4, 1024)
        b, n, _ = h.shape

        def split_heads(x):
            return x.reshape(b, n, NUM_HEADS, D_HEAD).transpose(0, 2, 1, 3)
        q = split_heads(h @ Wq.T + bq)
        k = split_heads(h @ Wk.T + bk)
        v = split_heads(h @ Wv.T + bv)
        scale = 1.0 / np.sqrt(D_HEAD)
        scores = jnp.einsum('bhqd,bhkd->bhqk', q, k) * scale
        mask = (adj == 0)[None, None, :, :]
        scores = jnp.where(mask, -jnp.inf, scores)
        attn = jax.nn.softmax(scores, axis=-1)
        out = jnp.einsum('bhqk,bhkd->bhqd', attn, v)
        out = out.transpose(0, 2, 1, 3).reshape(b, n, D_MODEL)
        return out @ Wo.T + bo

    def _L1_gnn_ref(x, adj, W, b):
        import jax, jax.numpy as jnp
        import numpy as np
        B, K, DIN, DOUT = (32, 64, 256, 256)
        Din = x.shape[-1]
        Wi, Wj = (W[:, :Din], W[:, Din:])
        mi = jnp.einsum('bkd,od->bko', x, Wi)
        mj = jnp.einsum('bkd,od->bko', x, Wj)
        a = adj.astype(x.dtype)
        deg = a.sum(axis=1)
        out = deg[None, :, None] * (mi + b) + jnp.einsum('ij,bjo->bio', a, mj)
        return out
    x = _layernorm(x + _L0_gnn_ref(x, adj, L0_gnn_Wq, L0_gnn_bq, L0_gnn_Wk, L0_gnn_bk, L0_gnn_Wv, L0_gnn_bv, L0_gnn_Wo, L0_gnn_bo), axis=-1)
    x = _layernorm(x + _L1_gnn_ref(x, adj, L1_gnn_W, L1_gnn_b), axis=-1)
    return x

_drawn_inputs = setup_inputs


def setup_inputs(seed=0):
    import zlib

    import numpy as np

    out = dict(_drawn_inputs(seed))
    spreads = {}
    factors = {'L0_gnn_bq': 31.341, 'L0_gnn_bk': 64.0}
    for name, (base, spread) in spreads.items():
        noise = np.random.default_rng([zlib.crc32(name.encode()), seed]).standard_normal(out[name].shape)
        drawn = base * np.exp(spread * noise) if base else spread * noise
        out[name] = jnp.asarray(drawn.astype(out[name].dtype))
    for name, factor in factors.items():
        out[name] = (out[name] * factor).astype(out[name].dtype)
    return out
```

```python
from contextlib import ExitStack

import concourse.bass as bass
from concourse import mybir

F32 = mybir.dt.float32
F32R = mybir.dt.float32r
BF16 = mybir.dt.bfloat16
I32 = mybir.dt.int32
ALU = mybir.AluOpType
ACT = mybir.ActivationFunctionType
AXX = mybir.AxisListType.X

P = 128
NB, N, D = 8, 1024, 256
H, DH = 8, 32
HG = P // DH
G = H // HG
NT = N // P
DC = D // P
HALF = 512
UNITS = HG * NT
LAG = 3
RING = 4
MASKED = 1e30
EPS = 1e-5
SCALE = 1.0 / DH ** 0.5
STACKS = HG * (P // DH)
PIECES = (("q", 0), ("q", 1), ("k", 0), ("k", 1), ("v", 0), ("v", 1))
PIECE_STEPS = (9, 12, 15, 17, 20, 23)
WO_STEPS = (3, 4, 5, 7)
STAT_STEP, EPS_STEP, NORM_STEP = 8, 17, 19
DRAIN = NORM_STEP + NT


def units_before(b, g, u):
    return b * (G * UNITS) + (g * UNITS + u)


def queries_before(b, g, q):
    return b * (G * NT) + (g * NT + q)


def misc_users(g, first, last, drain):
    users = [(u, "r", (u - 6) // 4) for u in range(2, UNITS, 4)
             if not (first and g == 0 and u < 6) and not (drain and u >= 6)]
    if g == 0 and not first:
        users += [(u, "wo", p) for p, u in enumerate(WO_STEPS)]
    if not (last and g == 1) and not drain:
        users += [(u, "pre", i) for i, u in enumerate(PIECE_STEPS)]
    return sorted(users)


def attention_phase(nc, x, xT, adj, wqT, wkT, wvT, woT, bq, bk, bv, bo, ident_in, x1, deg):
    with ExitStack() as ctx:
        def sb(name, shape, dt=F32):
            return ctx.enter_context(nc.sbuf_tensor(name, shape, dt))

        def sem(name):
            return ctx.enter_context(nc.semaphore(name))

        q_stack = [sb(f"q_stack{g}", [P, HG, N], F32R) for g in range(G)]
        k_stack = [sb(f"k_stack{g}", [P, HG, N], F32R) for g in range(G)]
        v_rows = [sb(f"v_rows{g}", [P, NT, P]) for g in range(G)]
        mask = sb("mask", [P, NT, N], BF16)
        ring = sb("ring", [P, RING, N])
        probsT = sb("probsT", [P, 2, HG, N])
        attnT = sb("attnT", [P, G, N])
        xT_sb = sb("xT_sb", [P, DC, N])
        x_sb = sb("x_sb", [P, NT, D])
        y_sb = sb("y_sb", [P, NT, D])
        full = sb("full", [P, 2, HALF])
        q_hi, q_lo = sb("q_hi", [P, N], F32R), sb("q_lo", [P, N], F32R)
        k_hi, k_lo = sb("k_hi", [P, N], F32R), sb("k_lo", [P, N], F32R)
        wq_sb, wk_sb, wv_sb, wo_sb = (sb(f"w{n}_sb", [P, DC, D]) for n in "qkvo")
        bq_sb, bk_sb, bq_c, bk_c = (sb(n, [P, G]) for n in ("bq_sb", "bk_sb", "bq_c", "bk_c"))
        bv_sb, bo_sb = sb("bv_sb", [P, D]), sb("bo_sb", [P, D])
        ident = sb("ident", [P, P])
        scratch = sb("scratch", [P, N], BF16)
        low = sb("low", [P, RING])
        sums = sb("sums", [P, 2, HG])
        recip = sb("recip", [P, HG])
        recip_cols = sb("recip_cols", [P, HG, DH])
        recipT = sb("recipT", [P, P])
        row_low, has_edge, has_inv, guard = (sb(n, [P, NT]) for n in ("row_low", "has_edge", "has_inv", "guard"))
        stats, moments = sb("stats", [P, NT, 6]), sb("moments", [P, NT, 2])
        var_eps, rstd, neg_half = (sb(n, [P, NT]) for n in ("var_eps", "rstd", "neg_half"))
        y_int = y_sb[:, :, :].bitcast(I32).rearrange("p (c t) d -> p c (t d)", c=2)

        scores = ctx.enter_context(nc.psum_tensor("scores", [P, 2, N], F32))
        turned = [ctx.enter_context(nc.psum_tensor(f"turned{j}", [P, HALF], F32)) for j in range(2)]
        pv = ctx.enter_context(nc.psum_tensor("pv", [P, HALF], F32))
        misc = ctx.enter_context(nc.psum_tensor("misc", [P, HALF], F32))

        weights_in = sem("weights_in")
        adj_in = [sem(f"adj_in{i}") for i in range(2)]
        xT_in, x_in = sem("xT_in"), sem("x_in")
        q_stacked, k_stacked = sem("q_stacked"), sem("k_stacked")
        x1_out = sem("x1_out")
        mask_made, deg_made, guard_step = sem("mask_made"), sem("deg_made"), sem("guard_step")
        bias_made, half_made = sem("bias_made"), sem("half_made")
        scored, lowered, probs_made = sem("scored"), sem("lowered"), sem("probs_made")
        turned_made = [sem(f"turned_made{j}") for j in range(2)]
        turned_kept = [sem(f"turned_kept{j}") for j in range(2)]
        pv_made, attn_made = sem("pv_made"), sem("attn_made")
        recip_made, cols_made, recipT_made, recipT_kept = sem("recip_made"), sem("cols_made"), sem("recipT_made"), sem("recipT_kept")
        qk_made, qk_kept, hi_made, lo_made = sem("qk_made"), sem("qk_kept"), sem("hi_made"), sem("lo_made")
        v_made, v_kept = sem("v_made"), sem("v_kept")
        dve_waited, sp_waited = sem("dve_waited"), sem("sp_waited")
        wo_made, wo_kept, x_biased = sem("wo_made"), sem("wo_kept"), sem("x_biased")
        stats_made, moments_made, eps_made, rstd_made, normed = sem("stats_made"), sem("moments_made"), sem("eps_made"), sem("rstd_made"), sem("normed")

        def kept(kind, i, b, g):
            if kind == "r":
                return recipT_kept, queries_before(b, g, i) + 1
            if kind == "wo":
                return wo_kept, (b - 1) * 4 + (i + 1)
            seg = b * G + (g + 1)
            return (qk_kept, seg * 4 + (i + 1)) if i < 4 else (v_kept, seg * 2 + (i - 3))

        def segments(eng, segment):
            for g in range(G):
                segment(0, g, True, False, False)
            with eng.Fori(1, NB - 1) as b:
                for g in range(G):
                    segment(b, g, False, False, False)
            for g in range(G):
                segment(NB - 1, g, False, True, False)
            segment(NB, 0, False, False, True)

        block = ctx.enter_context(nc.Block())

        @block.sync
        def _(sp):
            sp.sem_inc(x1_out, 16)
            for w, w_dram in ((wq_sb, wqT), (wk_sb, wkT)):
                sp.dma_start(w[:, :, :], w_dram.rearrange("(c p) n -> p c n", p=P)).then_inc(weights_in, 16)
            sp.dma_start(xT_sb[:, :, :], xT[0].rearrange("(c p) n -> p c n", p=P)).then_inc(xT_in, 16)
            for w, w_dram in ((wv_sb, wvT), (wo_sb, woT)):
                sp.dma_start(w[:, :, :], w_dram.rearrange("(c p) n -> p c n", p=P)).then_inc(weights_in, 16)
            for bias, b_dram in ((bq_sb, bq), (bk_sb, bk)):
                sp.dma_start(bias[:, :], b_dram).then_inc(weights_in, 16)
            for bias, b_dram in ((bv_sb, bv), (bo_sb, bo)):
                sp.dma_start(bias[:, :], b_dram.rearrange("(a n) -> a n", a=1).broadcast_to([P, D])).then_inc(weights_in, 16)
            sp.dma_start(ident[:, :], ident_in).then_inc(weights_in, 16)

            def load_adj(t):
                if t >= 2:
                    sp.wait_ge(mask_made, t - 1)
                    sp.wait_ge(deg_made, t - 1)
                sp.dma_start(y_int[:, t % 2, :], adj[t * P:(t + 1) * P, :]).then_inc(adj_in[t % 2], 16)

            load_adj(0)
            load_adj(1)

            def stack(seg, g, free):
                for parts, dst, landed, i in (((q_hi, q_lo, q_hi, q_lo), q_stack[g], q_stacked, 2),
                                              ((k_hi, k_hi, k_lo, k_lo), k_stack[g], k_stacked, 4)):
                    sp.wait_ge(lo_made, seg * 4 + i)
                    sp.sem_inc(sp_waited, 1)
                    if free is not None:
                        sp.wait_ge(scored, free)
                    for h in range(HG):
                        for j, part in enumerate(parts):
                            sp.dma_start(dst[j * DH:(j + 1) * DH, h, :].bitcast(F32), part[h * DH:(h + 1) * DH, :].bitcast(F32)).then_inc(landed, 16)

            stack(0, 0, None)

            def segment(b, g, first, last, drain):
                if g == 0 and not drain:
                    if not first:
                        sp.wait_ge(wo_kept, b * 4)
                    sp.sem_inc(sp_waited, 1)
                    sp.dma_start(x_sb[:, :, :], x[b].rearrange("(t p) d -> p t d", p=P)).then_inc(x_in, 16)
                    for t in range(2, NT if first else 2):
                        load_adj(t)
                if not (last and g == 1) and not drain:
                    stack(b * G + (g + 1), 1 - g, None if first and g == 0 else units_before(b, g, 0))
                if g == 0 and not last and not drain:
                    sp.wait_ge(v_made, (b * G + 2) * 2)
                    sp.sem_inc(sp_waited, 1)
                    sp.wait_ge(qk_made, (b * G + 2) * 4)
                    sp.sem_inc(sp_waited, 1)
                    sp.dma_start(xT_sb[:, :, :], xT[b + 1].rearrange("(c p) n -> p c n", p=P)).then_inc(xT_in, 16)
                if g == 0 and not first:
                    sp.wait_ge(normed, b * NT)
                    sp.sem_inc(sp_waited, 1)
                    sp.dma_start(x1[b - 1].rearrange("(t p) d -> p t d", p=P), y_sb[:, :, :]).then_inc(x1_out, 16)

            segments(sp, segment)
            sp.wait_ge(x1_out, (NB + 1) * 16)

        @block.gpsimd
        def _(pool):
            pool.memset(neg_half[:, :], -0.5).then_inc(half_made, 1)
            pool.wait_ge(half_made, 1)
            pool.wait_ge(weights_in, 9 * 16)

            def batch(b):
                pool.wait_ge(x_in, b * 16 + 16)
                pool.tensor_tensor(x_sb[:, :, :], x_sb[:, :, :], bo_sb[:, :].unsqueeze(1).broadcast_to([P, NT, D]),
                                   ALU.add).then_inc(x_biased, 1)
                pool.wait_ge(eps_made, b + 1)
                pool.tensor_tensor(rstd[:, :], var_eps[:, :], neg_half[:, :], ALU.pow).then_inc(rstd_made, 1)

            with pool.Fori(0, NB) as b:
                batch(b)

        @block.scalar
        def _(act):
            act.wait_ge(bias_made, 2)

            def project(seg, i, reused):
                kind, half = PIECES[i]
                act.wait_ge(qk_made, seg * 4 + (i + 1))
                if reused or i >= 2:
                    act.wait_ge(lo_made, seg * 4 + (i - 1))
                hi, bias, scale, landed = (q_hi, bq_c, SCALE, q_stacked) if kind == "q" else (k_hi, bk_c, -1.0, k_stacked)
                gg = project.group
                act.activation(full[:, half, :], misc[:, :], ACT.Identity, bias=bias[:, gg:gg + 1], scale=scale).then_inc(qk_kept, 1)
                act.wait_ge(qk_kept, seg * 4 + (i + 1))
                if reused and half == 0:
                    act.wait_ge(landed, seg * (STACKS * 16))
                act.activation(hi[:, half * HALF:(half + 1) * HALF], full[:, half, :], ACT.Copy).then_inc(hi_made, 1)

            project.group = 0
            def degree(t):
                act.wait_ge(adj_in[t % 2], (t // 2 + 1) * 16)
                if t > 0:
                    act.wait_ge(deg_made, t)
                act.activation(scratch[:, :], y_int[:, t % 2, :], ACT.Copy, accum_out=deg[:, t:t + 1]).then_inc(deg_made, 1)

            degree(0)
            degree(1)
            for i in range(4):
                project(0, i, False)

            def segment(b, g, first, last, drain):
                pre_steps = {} if drain or (last and g == 1) else {u + 1: i for i, u in enumerate(PIECE_STEPS) if i < 4}
                opening = first and g == 0
                for u in range(LAG + 5 if drain else UNITS):
                    t = u - LAG
                    if not (opening and t < 0) and not (drain and t >= 0):
                        act.wait_ge(turned_made[0], units_before(b, g, t) + 1)
                        if t % HG == 0 and not (opening and t < 2 * HG):
                            act.wait_ge(pv_made, queries_before(b, g, t // HG - 1))
                        act.activation(probsT[:, t // HG % 2, t % HG, 0:HALF], turned[0][:, :], ACT.Copy).then_inc(turned_kept[0], 1)
                    q = (u - 7) // HG
                    if u % HG == 3 and not (opening and q < 0) and not (drain and q >= 0):
                        act.wait_ge(recipT_made, queries_before(b, g, q) + 1)
                        if not (opening and q < 1):
                            act.wait_ge(attn_made, queries_before(b, g, q))
                        act.activation(recipT[:, :], misc[:, 0:P], ACT.Copy).then_inc(recipT_kept, 1)
                    if u in pre_steps:
                        project.group = 1 - g
                        project(b * G + (g + 1), pre_steps[u], True)
                    if (u == 0 or not drain) and not (opening and u == 0):
                        e = u - 1
                        act.wait_ge(lowered, units_before(b, g, u))
                        act.activation(ring[:, e % RING, :], ring[:, e % RING, :], ACT.Exp, bias=low[:, e % RING:e % RING + 1],
                                       scale=-1.0, accum_out=sums[:, e // HG % 2, e % HG:e % HG + 1]).then_inc(probs_made, 1)
                    if opening and u % HG == 1 and u // HG + 2 < NT:
                        degree(u // HG + 2)

            segments(act, segment)

        @block.vector
        def _(dve):
            dve.wait_ge(weights_in, 9 * 16)
            nc.vector.tensor_scalar(bq_c[:, :], bq_sb[:, :], SCALE, None, ALU.mult).then_inc(bias_made, 1)
            nc.vector.tensor_scalar(bk_c[:, :], bk_sb[:, :], -1.0, None, ALU.mult).then_inc(bias_made, 1)

            def low_part(seg, i, reused):
                kind, half = PIECES[i]
                hi, lo, landed = (q_hi, q_lo, q_stacked) if kind == "q" else (k_hi, k_lo, k_stacked)
                cols = slice(half * HALF, (half + 1) * HALF)
                dve.wait_ge(hi_made, seg * 4 + (i + 1))
                if reused and half == 0:
                    dve.wait_ge(landed, seg * (STACKS * 16))
                nc.vector.tensor_tensor(lo[:, cols], full[:, half, :], hi[:, cols].bitcast(F32), ALU.subtract).then_inc(lo_made, 1)

            def keep_v(seg, g, i, free):
                dve.wait_ge(v_made, seg * 2 + (i + 1))
                if free is not None:
                    dve.wait_ge(pv_made, free)
                nc.vector.tensor_tensor(v_rows[g][:, 4 * i:4 * i + 4, :], misc[:, :].rearrange("p (t n) -> p t n", t=4),
                                        bv_sb[:, g * P:(g + 1) * P].unsqueeze(1).broadcast_to([P, 4, P]), ALU.add).then_inc(v_kept, 1)

            def make_mask(t):
                dve.wait_ge(adj_in[t % 2], (t // 2 + 1) * 16)
                nc.vector.tensor_scalar(mask[:, t, :], y_int[:, t % 2, :], 0, MASKED, ALU.is_equal, ALU.mult).then_inc(mask_made, 1)

            def make_guard(t):
                row = slice(t, t + 1)
                dve.wait_ge(mask_made, t + 1)
                nc.vector.tensor_reduce(row_low[:, row], mask[:, t, :], AXX, ALU.min).then_inc(guard_step, 1)
                dve.wait_ge(guard_step, 4 * t + 1)
                nc.vector.tensor_scalar(has_edge[:, row], row_low[:, row], 0.0, None, ALU.is_equal).then_inc(guard_step, 1)
                dve.wait_ge(guard_step, 4 * t + 2)
                nc.vector.reciprocal(has_inv[:, row], has_edge[:, row]).then_inc(guard_step, 1)
                dve.wait_ge(guard_step, 4 * t + 3)
                nc.vector.tensor_tensor(guard[:, row], has_edge[:, row], has_inv[:, row], ALU.mult).then_inc(guard_step, 1)

            make_mask(0)
            make_mask(1)
            for i in range(4):
                low_part(0, i, False)
            for i in range(2):
                keep_v(0, 0, i, None)

            def segment(b, g, first, last, drain):
                opening = first and g == 0
                pre = not drain and not (last and g == 1)
                pre_steps = {u + 1: i for i, u in enumerate(PIECE_STEPS)} if pre else {}
                wo_steps = {u + 1: p for p, u in enumerate(WO_STEPS)} if g == 0 and not first else {}
                post = g == 0 and not first
                for u in range(DRAIN if drain else UNITS):
                    q = (u - 11) // HG
                    if u % HG == 3 and not (opening and q < 0) and not (drain and q >= 0):
                        gq = g if q >= 0 else 1 - g
                        t = q % NT
                        dve.wait_ge(pv_made, queries_before(b, g, q) + 1)
                        dve.wait_ge(recipT_kept, queries_before(b, g, q) + 1)
                        if not first and q >= 0:
                            dve.wait_ge(wo_made, (b - 1) * 4 + (t // 2 + 1))
                        nc.vector.tensor_tensor(attnT[:, gq, t * P:(t + 1) * P], pv[:, 0:P], recipT[:, :], ALU.mult).then_inc(attn_made, 1)
                    if post and STAT_STEP < u <= STAT_STEP + NT:
                        dve.wait_ge(stats_made, (b - 1) * NT + (u - STAT_STEP))
                    e = u - 1
                    if (u == 0 or not drain) and not (opening and u == 0):
                        dve.wait_ge(scored, units_before(b, g, e) + 1)
                        if not (opening and e < RING):
                            dve.wait_ge(turned_made[1], units_before(b, g, e) - (RING - 1))
                        if opening and e % HG == 0:
                            dve.wait_ge(mask_made, e // HG + 1)
                        dve.sem_inc(dve_waited, 1)
                        nc.vector.tensor_tensor_reduce(ring[:, e % RING, :], scores[:, e % 2, :], mask[:, e // HG % NT, :], 1.0, 3e38,
                                                       ALU.add, ALU.min, low[:, e % RING:e % RING + 1]).then_inc(lowered, 1)
                    t = u - LAG
                    if not (opening and t < 0) and not (drain and t >= 0):
                        dve.wait_ge(turned_made[1], units_before(b, g, t) + 1)
                        if t % HG == 0 and not (opening and t < 2 * HG):
                            dve.wait_ge(pv_made, queries_before(b, g, t // HG - 1))
                        nc.vector.tensor_copy(probsT[:, t // HG % 2, t % HG, HALF:N], turned[1][:, :]).then_inc(turned_kept[1], 1)
                    if opening and u % HG == 1 and u // HG + 2 < NT:
                        make_mask(u // HG + 2)
                    if opening and u % HG == 2:
                        make_guard(u // HG)
                        if u // HG == NT - 1:
                            dve.wait_ge(guard_step, 4 * NT)
                    q = (u - 5) // HG
                    if u % HG == 1 and not (opening and q < 0) and not (drain and q >= 0):
                        t = q % NT
                        dve.wait_ge(probs_made, units_before(b, g, HG * q + HG))
                        nc.vector.reciprocal(recip[:, :], sums[:, q % 2, :]).then_inc(recip_made, 1)
                        dve.wait_ge(recip_made, queries_before(b, g, q) + 1)
                        if not (opening and q < 1):
                            dve.wait_ge(recipT_made, queries_before(b, g, q))
                        if opening:
                            dve.wait_ge(guard_step, 4 * t + 4)
                        nc.vector.tensor_scalar(recip_cols[:, :, :], recip[:, :].unsqueeze(2).broadcast_to([P, HG, DH]),
                                                guard[:, t:t + 1], None, ALU.mult).then_inc(cols_made, 1)
                    if u in pre_steps:
                        i = pre_steps[u]
                        if i < 4:
                            low_part(b * G + (g + 1), i, True)
                        else:
                            keep_v(b * G + (g + 1), 1 - g, i - 4, None if opening else queries_before(b, g, 0))
                    if u in wo_steps:
                        p = wo_steps[u]
                        dve.wait_ge(wo_made, (b - 1) * 4 + (p + 1))
                        if p == 0:
                            dve.wait_ge(x_biased, b)
                            dve.wait_ge(x1_out, b * 16)
                        nc.vector.tensor_tensor(y_sb[:, 2 * p:2 * p + 2, :], misc[:, :].rearrange("p (t n) -> p t n", t=2),
                                                x_sb[:, 2 * p:2 * p + 2, :], ALU.add).then_inc(wo_kept, 1)
                    if post and STAT_STEP <= u < STAT_STEP + NT:
                        t = u - STAT_STEP
                        dve.wait_ge(wo_kept, (b - 1) * 4 + (t // 2 + 1))
                        nc.vector.bn_stats(stats[:, t, :], y_sb[:, t, :]).then_inc(stats_made, 1)
                    if post and STAT_STEP < u <= STAT_STEP + NT:
                        t = u - STAT_STEP - 1
                        nc.vector.bn_aggr(moments[:, t, :], stats[:, t, :]).then_inc(moments_made, 1)
                    if post and u == EPS_STEP:
                        dve.wait_ge(moments_made, b * NT)
                        nc.vector.tensor_scalar(var_eps[:, :], moments[:, :, 1], EPS, None, ALU.add).then_inc(eps_made, 1)
                    if post and NORM_STEP <= u < NORM_STEP + NT:
                        t = u - NORM_STEP
                        dve.wait_ge(rstd_made, b)
                        nc.vector.tensor_scalar(y_sb[:, t, :], y_sb[:, t, :], moments[:, t, 0:1], rstd[:, t:t + 1],
                                                ALU.subtract, ALU.mult).then_inc(normed, 1)

            segments(dve, segment)

        @block.tensor
        def _(pe):
            pe.wait_ge(weights_in, 9 * 16)
            pe.wait_ge(xT_in, 16)

            def project(seg, g, i):
                kind, half = PIECES[i]
                if kind == "v":
                    for t in range(4):
                        rows = slice((4 * half + t) * P, (4 * half + t + 1) * P)
                        for c in range(DC):
                            last = nc.tensor.matmul(misc[:, t * P:(t + 1) * P], xT_sb[:, c, rows], wv_sb[:, c, g * P:(g + 1) * P],
                                                    start=(c == 0), stop=(c == DC - 1))
                    last.then_inc(v_made, 1)
                else:
                    w = wq_sb if kind == "q" else wk_sb
                    for c in range(DC):
                        last = nc.tensor.matmul(misc[:, :], w[:, c, g * P:(g + 1) * P], xT_sb[:, c, half * HALF:(half + 1) * HALF],
                                                start=(c == 0), stop=(c == DC - 1))
                    last.then_inc(qk_made, 1)

            for i in range(len(PIECES)):
                if i > 0:
                    pe.wait_ge(*kept("pre", i - 1, -1, G - 1))
                project(0, 0, i)

            def segment(b, g, first, last, drain):
                opening = first and g == 0
                users = misc_users(g, first, last, drain)
                for u in range(LAG + 8 if drain else UNITS):
                    t = u - LAG
                    turn = not (opening and t < 0) and not (drain and t >= 0)
                    for j in range(2):
                        if turn:
                            if j == 0:
                                pe.wait_ge(probs_made, units_before(b, g, t) + 1)
                            if not (opening and t < 1):
                                pe.wait_ge(turned_kept[j], units_before(b, g, t))
                            for c in range(4):
                                k = 4 * j + c
                                mm = nc.tensor.transpose(turned[j][:, c * P:(c + 1) * P], ring[:, t % RING, k * P:(k + 1) * P], ident[:, :])
                            mm.then_inc(turned_made[j], 1)
                        if not drain:
                            if j == 0:
                                if not (opening and u < 2):
                                    pe.wait_ge(lowered, units_before(b, g, u) - 1)
                                if u == 0:
                                    pe.wait_ge(q_stacked, (b * G + (g + 1)) * (STACKS * 16))
                                    pe.wait_ge(k_stacked, (b * G + (g + 1)) * (STACKS * 16))
                            h, q = u % HG, u // HG
                            mm = nc.tensor.matmul(scores[:, u % 2, j * HALF:(j + 1) * HALF], q_stack[g][:, h, q * P:(q + 1) * P],
                                                  k_stack[g][:, h, j * HALF:(j + 1) * HALF], start=True, stop=True)
                            if j == 1:
                                mm.then_inc(scored, 1)
                    q, c = (u - 7) // HG, (u - 7) % HG
                    if not (opening and q < 0) and not (drain and q >= 0):
                        gq = g if q >= 0 else 1 - g
                        if c == 0:
                            for j in range(2):
                                pe.wait_ge(turned_kept[j], units_before(b, g, HG * q + HG))
                            if not (opening and q < 1):
                                pe.wait_ge(attn_made, queries_before(b, g, q))
                            if q == 0:
                                pe.wait_ge(v_kept, (b * G + (g + 1)) * 2)
                        for k in (2 * c, 2 * c + 1):
                            for h in range(HG):
                                mm = nc.tensor.matmul(pv[h * DH:(h + 1) * DH, 0:P], v_rows[gq][:, k, h * DH:(h + 1) * DH],
                                                      probsT[:, q % 2, h, k * P:(k + 1) * P], start=(k == 0), stop=(k == NT - 1))
                        if c == HG - 1:
                            mm.then_inc(pv_made, 1)
                    for n, (at, kind, i) in enumerate(users):
                        if at != u:
                            continue
                        if n > 0:
                            pe.wait_ge(*kept(*users[n - 1][1:], b, g))
                        elif not opening:
                            pe.wait_ge(recipT_kept, queries_before(b, g, i))
                        else:
                            pe.wait_ge(v_kept, 2)
                        if kind == "r":
                            pe.wait_ge(cols_made, queries_before(b, g, i) + 1)
                            nc.tensor.transpose(misc[:, 0:P], recip_cols[:, :, :].rearrange("p h d -> p (h d)"), ident[:, :]).then_inc(recipT_made, 1)
                        elif kind == "wo":
                            pe.wait_ge(attn_made, queries_before(b - 1, 1, 2 * i + 2))
                            for j in range(2):
                                rows = slice((2 * i + j) * P, (2 * i + j + 1) * P)
                                for c in range(G):
                                    mm = nc.tensor.matmul(misc[:, j * D:(j + 1) * D], attnT[:, c, rows], wo_sb[:, c, :],
                                                          start=(c == 0), stop=(c == G - 1))
                            mm.then_inc(wo_made, 1)
                        else:
                            if g == 1 and i == 0:
                                pe.wait_ge(xT_in, b * 16 + 32)
                            project(b * G + (g + 1), 1 - g, i)

            segments(pe, segment)


def convolution_phase(nc, adjT, wijT, bias, ident_in, x1, deg, out):
    with ExitStack() as ctx:
        def sb(name, shape, dt=F32):
            return ctx.enter_context(nc.sbuf_tensor(name, shape, dt))

        def sem(name):
            return ctx.enter_context(nc.semaphore(name))

        edges = sb("edges", [P, NT, N], F32R)
        edges_int = sb("edges_int", [P, NT, N], I32)
        w_sb = sb("w_sb", [P, DC, 2 * D])
        bias_sb = sb("bias_sb", [P, D])
        deg_bias = sb("deg_bias", [P, NT, D])
        ident = sb("ident2", [P, P])
        x1_sb = sb("x1_sb", [P, 2, NT, D])
        x1T = sb("x1T", [P, DC, N])
        x1_bias = sb("x1_bias", [P, NT, D])
        msg = sb("msg", [P, NT, 2 * D], F32R)
        own = sb("own", [P, NT, D])
        y_sb = sb("y2_sb", [P, 2, NT, D])
        stats, moments = sb("stats2", [P, NT, 6]), sb("moments2", [P, NT, 2])
        var_eps, rstd, neg_half = (sb(n, [P, NT]) for n in ("var_eps2", "rstd2", "neg_half2"))

        mlp = ctx.enter_context(nc.psum_tensor("mlp", [P, 2, 2 * D], F32))
        agg = ctx.enter_context(nc.psum_tensor("agg", [P, 2, 2 * D], F32))
        turned = ctx.enter_context(nc.psum_tensor("turned", [P, 2, HALF], F32))

        weights_in, adj_in = sem("weights_in2"), sem("adj_in_t")
        dve_waited, sp_waited = sem("dve_waited2"), sem("sp_waited2")
        x1_in = [sem(f"x1_in{k}") for k in range(2)]
        out_sent = [sem(f"out_sent{k}") for k in range(2)]
        edges_made, deg_bias_made, half_made, x1_biased = sem("edges_made"), sem("deg_bias_made"), sem("half_made2"), sem("x1_biased")
        turned_made, turned_kept = sem("turned_made"), sem("turned_kept")
        mlp_made, hi_made, lo_made, own_made = sem("mlp_made"), sem("hi_made2"), sem("lo_made2"), sem("own_made")
        agg_made, half_added, agg_kept = sem("agg_made"), sem("half_added"), sem("agg_kept")
        stats_made, moments_made, eps_made, rstd_made, normed = sem("stats_made2"), sem("moments_made2"), sem("eps_made2"), sem("rstd_made2"), sem("normed2")

        def batches(eng, batch):
            for k in range(2):
                batch(k, k, k == 0, False)
            with eng.Fori(1, NB // 2 - 1) as pair:
                for k in range(2):
                    batch(pair * 2 + k, k, False, False)
            for k in range(2):
                batch(NB - 2 + k, k, False, k == 1)

        block = ctx.enter_context(nc.Block())

        @block.sync
        def _(sp):
            sp.dma_start(x1_sb[:, 0, :, :], x1[0].rearrange("(t p) d -> p t d", p=P)).then_inc(x1_in[0], 16)
            sp.dma_start(ident[:, :], ident_in).then_inc(weights_in, 16)
            sp.dma_start(w_sb[:, :, :], wijT.rearrange("(c p) n -> p c n", p=P)).then_inc(weights_in, 16)
            sp.dma_start(bias_sb[:, :], bias.rearrange("(a n) -> a n", a=1).broadcast_to([P, D])).then_inc(weights_in, 16)
            sp.dma_start(edges_int[:, :, :], adjT.rearrange("(t p) n -> p t n", p=P)).then_inc(adj_in, 16)

            def batch(b, k, first, last):
                if not last:
                    if not first:
                        sp.wait_ge(own_made, b * NT)
                    sp.sem_inc(sp_waited, 1)
                    sp.dma_start(x1_sb[:, 1 - k, :, :], x1[b + 1].rearrange("(t p) d -> p t d", p=P)).then_inc(x1_in[1 - k], 16)
                sp.wait_ge(normed, b * NT + NT)
                sp.sem_inc(sp_waited, 1)
                sp.dma_start(out[b].rearrange("(t p) d -> p t d", p=P), y_sb[:, k, :, :]).then_inc(out_sent[k], 16)

            batches(sp, batch)
            for k in range(2):
                sp.wait_ge(out_sent[k], NB // 2 * 16)

        @block.gpsimd
        def _(pool):
            nc.gpsimd.memset(neg_half[:, :], -0.5).then_inc(half_made, 1)
            pool.wait_ge(half_made, 1)

            def batch(b, k, first, last):
                for t in range(NT):
                    pool.wait_ge(eps_made, b * NT + (t + 1))
                    nc.gpsimd.tensor_tensor(rstd[:, t:t + 1], var_eps[:, t:t + 1], neg_half[:, t:t + 1], ALU.pow).then_inc(rstd_made, 1)

            batches(pool, batch)

        @block.scalar
        def _(act):
            act.wait_ge(adj_in, 16)
            for t in range(NT):
                act.activation(edges[:, t, :], edges_int[:, t, :], ACT.Copy).then_inc(edges_made, 1)

            def keep_turned(turn, i):
                act.wait_ge(turned_made, turn * 4 + (i + 1))
                nc.scalar.activation(x1T[:, :, 2 * i * P:(2 * i + 2) * P], turned[:, i % 2, :].rearrange("p (c n) -> p c n", c=DC),
                                     ACT.Copy).then_inc(turned_kept, 1)

            for i in range(4):
                keep_turned(0, i)

            def batch(b, k, first, last):
                for t in range(NT):
                    act.wait_ge(mlp_made, b * NT + (t + 1))
                    if t == 0 and not first:
                        act.wait_ge(agg_made, b * NT)
                    nc.scalar.activation(msg[:, t, 0:D], mlp[:, t % 2, D:2 * D], ACT.Copy).then_inc(hi_made, 1)
                if not last:
                    for i in range(4):
                        keep_turned(b + 1, i)

            batches(act, batch)

        @block.vector
        def _(dve):
            dve.wait_ge(weights_in, 48)
            for t in range(NT):
                nc.vector.tensor_scalar(deg_bias[:, t, :], bias_sb[:, :], deg[:, t:t + 1], None, ALU.mult).then_inc(deg_bias_made, 1)
            dve.wait_ge(deg_bias_made, NT)

            def batch(b, k, first, last):
                dve.wait_ge(x1_in[k], (b - k) * 8 + 16)
                nc.vector.tensor_tensor(x1_bias[:, :, :], x1_sb[:, k, :, :], deg_bias[:, :, :], ALU.add).then_inc(x1_biased, 1)
                dve.wait_ge(x1_biased, b + 1)
                for t in range(NT):
                    dve.wait_ge(hi_made, b * NT + (t + 1))
                    nc.vector.tensor_tensor(msg[:, t, D:2 * D], mlp[:, t % 2, D:2 * D], msg[:, t, 0:D].bitcast(F32),
                                            ALU.subtract).then_inc(lo_made, 1)
                    nc.vector.scalar_tensor_tensor(out=own[:, t, :], in0=mlp[:, t % 2, 0:D], scalar=deg[:, t:t + 1],
                                                   in1=x1_bias[:, t, :], op0=ALU.mult, op1=ALU.add).then_inc(own_made, 1)

                def norm(t):
                    dve.wait_ge(rstd_made, b * NT + (t + 1))
                    nc.vector.tensor_scalar(y_sb[:, k, t, :], y_sb[:, k, t, :], moments[:, t, 0:1], rstd[:, t:t + 1],
                                            ALU.subtract, ALU.mult).then_inc(normed, 1)

                dve.wait_ge(own_made, b * NT + NT)
                if isinstance(b, int) and b < 2:
                    pass
                else:
                    dve.wait_ge(out_sent[k], (b - k) * 8)
                for t in range(NT):
                    done = b * NT + (t + 1)
                    dve.wait_ge(agg_made, done)
                    nc.vector.tensor_tensor(y_sb[:, k, t, :], agg[:, t % 2, 0:D], own[:, t, :], ALU.add).then_inc(half_added, 1)
                    dve.wait_ge(half_added, done)
                    nc.vector.tensor_tensor(y_sb[:, k, t, :], agg[:, t % 2, D:2 * D], y_sb[:, k, t, :], ALU.add).then_inc(agg_kept, 1)
                    dve.wait_ge(agg_kept, done)
                    nc.vector.bn_stats(stats[:, t, :], y_sb[:, k, t, :]).then_inc(stats_made, 1)
                    dve.wait_ge(stats_made, done)
                    dve.sem_inc(dve_waited, 1)
                    nc.vector.bn_aggr(moments[:, t, :], stats[:, t, :]).then_inc(moments_made, 1)
                    dve.wait_ge(moments_made, done)
                    nc.vector.tensor_scalar(var_eps[:, t:t + 1], moments[:, t, 1:2], EPS, None, ALU.add).then_inc(eps_made, 1)
                    if t >= 2:
                        norm(t - 2)
                norm(NT - 2)
                norm(NT - 1)

            batches(dve, batch)

        @block.tensor
        def _(pe):
            pe.wait_ge(weights_in, 48)

            def turn(turn, k, i, at_start):
                if i == 0:
                    pe.wait_ge(x1_in[k], (turn - k) * 8 + 16)
                if not (at_start and i < 2):
                    pe.wait_ge(turned_kept, turn * 4 + (i - 1))
                for j in range(2):
                    for c in range(DC):
                        mm = nc.tensor.transpose(turned[:, i % 2, c * D + j * P:c * D + (j + 1) * P],
                                                 x1_sb[:, k, 2 * i + j, c * P:(c + 1) * P], ident[:, :])
                mm.then_inc(turned_made, 1)

            for i in range(4):
                turn(0, 0, i, True)

            def batch(b, k, first, last):
                for t in range(NT):
                    if t % 2 == 0:
                        pe.wait_ge(turned_kept, b * 4 + (t // 2 + 1))
                    if t >= 2:
                        pe.wait_ge(own_made, b * NT + (t - 1))
                    elif not first:
                        pe.wait_ge(own_made, b * NT)
                    for c in range(DC):
                        mm = nc.tensor.matmul(mlp[:, t % 2, :], x1T[:, c, t * P:(t + 1) * P], w_sb[:, c, :],
                                              start=(c == 0), stop=(c == DC - 1))
                    mm.then_inc(mlp_made, 1)
                pe.wait_ge(edges_made, NT)
                pe.wait_ge(lo_made, b * NT + NT)
                pe.wait_ge(hi_made, b * NT + NT)
                for t in range(NT):
                    if t >= 2:
                        pe.wait_ge(agg_kept, b * NT + (t - 1))
                    elif not first:
                        pe.wait_ge(agg_kept, b * NT)
                    for j in range(NT):
                        mm = nc.tensor.matmul(agg[:, t % 2, :], edges[:, j, t * P:(t + 1) * P], msg[:, j, :],
                                              start=(j == 0), stop=(j == NT - 1))
                    mm.then_inc(agg_made, 1)
                    if t % 2 == 1 and not last:
                        turn(b + 1, 1 - k, t // 2, False)

            batches(pe, batch)


def build(nc, x, xT, adj, adjT, ident, wqT, bq, wkT, bk, wvT, bv, woT, bo, wijT, bias, out):
    x1 = nc.dram_tensor("x1_dram", (NB, N, D), F32, kind="Internal").ap()
    with nc.sbuf_tensor("deg", [P, NT], F32) as deg:
        attention_phase(nc, x, xT, adj, wqT, wkT, wvT, woT, bq, bk, bv, bo, ident, x1, deg)
        convolution_phase(nc, adjT, wijT, bias, ident, x1, deg, out)


def kernel(x, adj, L0_gnn_Wq, L0_gnn_bq, L0_gnn_Wk, L0_gnn_bk, L0_gnn_Wv, L0_gnn_bv, L0_gnn_Wo, L0_gnn_bo, L1_gnn_W, L1_gnn_b):
    import numpy as np
    import concourse.bacc as bacc
    from concourse.bass_utils import run_bass_kernel_spmd

    def laid(a):
        return np.ascontiguousarray(a)

    x, adj, w1 = np.asarray(x), np.asarray(adj), np.asarray(L1_gnn_W)
    arrays = {
        "x": laid(x), "xT": laid(x.transpose(0, 2, 1)), "adj": laid(adj), "adjT": laid(adj.T),
        "ident": np.eye(P, dtype=np.float32),
        "wqT": laid(np.asarray(L0_gnn_Wq).T), "bq": laid(np.asarray(L0_gnn_bq).reshape(G, P).T), "wkT": laid(np.asarray(L0_gnn_Wk).T), "bk": laid(np.asarray(L0_gnn_bk).reshape(G, P).T),
        "wvT": laid(np.asarray(L0_gnn_Wv).T), "bv": laid(L0_gnn_bv), "woT": laid(np.asarray(L0_gnn_Wo).T), "bo": laid(L0_gnn_bo),
        "wijT": laid(w1.reshape(D, 2, D).transpose(2, 1, 0).reshape(D, 2 * D)), "bias": laid(L1_gnn_b),
    }
    nc = bacc.Bacc("TRN2", target_bir_lowering=False, num_devices=1)
    args = [nc.dram_tensor(n + "_dram", a.shape, mybir.dt.from_np(a.dtype), kind="ExternalInput").ap() for n, a in arrays.items()]
    out = nc.dram_tensor("out_dram", x.shape, F32, kind="ExternalOutput").ap()
    build(nc, *args, out)
    r = run_bass_kernel_spmd(nc, [{n + "_dram": a for n, a in arrays.items()}], core_ids=[0])
    return r.results[0]["out_dram"]
```

```python
from contextlib import ExitStack

import concourse.bass as bass
from concourse import mybir

F32 = mybir.dt.float32
F32R = mybir.dt.float32r
BF16 = mybir.dt.bfloat16
I32 = mybir.dt.int32
ALU = mybir.AluOpType
ACT = mybir.ActivationFunctionType
AXX = mybir.AxisListType.X

P = 128
NB, N, D = 8, 1024, 256
H, DH = 8, 32
HG = P // DH
G = H // HG
NT = N // P
DC = D // P
HALF = 512
UNITS = HG * NT
LAG = 3
ACT_BOTH = (0, 2)
RING = 4
MASKED = 1e30
EPS = 1e-5
SCALE = 1.0 / DH ** 0.5
STACKS = P // DH
PIECES = (("q", 0), ("q", 1), ("k", 0), ("k", 1), ("v", 0), ("v", 1))
PIECE_STEPS = (9, 12, 15, 17, 20, 23)
WO_STEPS = (3, 4, 5, 7)
STAT_STEP, EPS_STEP, NORM_STEP = 8, 17, 19
DRAIN = EPS_STEP + 1


def units_before(b, g, u):
    return b * (G * UNITS) + (g * UNITS + u)


def queries_before(b, g, q):
    return b * (G * NT) + (g * NT + q)


def misc_users(g, first, last, drain):
    users = [(u, "r", (u - 6) // 4) for u in range(2, UNITS, 4)
             if not (first and g == 0 and u < 6) and not (drain and u >= 6)]
    if g == 0 and not first:
        users += [(u, "wo", p) for p, u in enumerate(WO_STEPS)]
    if not (last and g == 1) and not drain:
        users += [(u, "pre", i) for i, u in enumerate(PIECE_STEPS)]
    return sorted(users)


def gnn_layers(nc, x, xT, adj, adjT, ident_in, wqT, bq, wkT, bk, wvT, bv, woT, bo, wijT, bias, x1, out):
    with ExitStack() as ctx:
        def sb(name, shape, dt=F32):
            return ctx.enter_context(nc.sbuf_tensor(name, shape, dt))

        def sem(name):
            return ctx.enter_context(nc.semaphore(name))

        q_stack = [sb(f"q_stack{g}", [P, HG, N], F32R) for g in range(G)]
        k_stack = [sb(f"k_stack{g}", [P, HG, N], F32R) for g in range(G)]
        v_rows = [sb(f"v_rows{g}", [P, NT, P]) for g in range(G)]
        mask = sb("mask", [P, NT, N], BF16)
        ring = sb("ring", [P, RING, N])
        probsT = sb("probsT", [P, 2, HG, N])
        attnT = sb("attnT", [P, G, N])
        xT_sb = sb("xT_sb", [P, DC, N])
        x_sb = sb("x_sb", [P, NT, D])
        y_sb = sb("y_sb", [P, NT, D])
        full = sb("full", [P, 2, HALF])
        q_hi, q_lo = sb("q_hi", [P, N], F32R), sb("q_lo", [P, N], F32R)
        k_hi, k_lo = sb("k_hi", [P, N], F32R), sb("k_lo", [P, N], F32R)
        wq_sb, wk_sb, wv_sb, wo_sb = (sb(f"w{n}_sb", [P, DC, D]) for n in "qkvo")
        bq_sb, bk_sb, bq_c, bk_c = (sb(n, [P, G]) for n in ("bq_sb", "bk_sb", "bq_c", "bk_c"))
        bv_sb, bo_sb, bias_sb = (sb(n, [P, D]) for n in ("bv_sb", "bo_sb", "bias_sb"))
        ident = sb("ident", [P, P])
        scratch = sb("scratch", [P, N], BF16)
        deg = sb("deg", [P, NT])
        low = sb("low", [P, RING])
        sums = sb("sums", [P, 2, HG])
        recip = sb("recip", [P, HG])
        recip_cols = sb("recip_cols", [P, HG, DH])
        recipT = sb("recipT", [P, P])
        row_low, has_edge, has_inv, guard = (sb(n, [P, NT]) for n in ("row_low", "has_edge", "has_inv", "guard"))
        stats, moments = sb("stats", [P, NT, 6]), sb("moments", [P, NT, 2])
        var_eps, rstd, neg_half = (sb(n, [P, NT]) for n in ("var_eps", "rstd", "neg_half"))
        y_int = y_sb[:, :, :].bitcast(I32).rearrange("p (c t) d -> p c (t d)", c=2)

        scores = ctx.enter_context(nc.psum_tensor("scores", [P, 2, N], F32))
        turned = [ctx.enter_context(nc.psum_tensor(f"turned{j}", [P, HALF], F32)) for j in range(2)]
        pv = ctx.enter_context(nc.psum_tensor("pv", [P, HALF], F32))
        misc = ctx.enter_context(nc.psum_tensor("misc", [P, HALF], F32))

        edges = [k_stack[t // HG][:, t % HG, :] for t in range(NT)]
        edges_int = [xT_sb[:, t, :].bitcast(I32) for t in range(2)] + [ring[:, t, :].bitcast(I32) for t in range(RING)]
        x1_sb = mask[:, :, :].bitcast(F32).rearrange("p (k t) (u d) -> p k (t u) d", k=2, u=2)
        x1T = attnT
        msg = q_stack[0][:, :, :].rearrange("p h (t n) -> p (h t) n", t=2)
        w_sb = full
        deg_bias = x_sb
        own, x1_bias, out_sb0, out_sb1 = (probsT[:, k // 2, 2 * (k % 2):2 * (k % 2) + 2, :].rearrange("p h (t d) -> p (h t) d", d=D)
                                          for k in range(4))
        out_sb = (out_sb0, out_sb1)
        mlp = scores[:, 0, :].rearrange("p (k n) -> p k n", k=2)
        agg = scores[:, 1, :].rearrange("p (k n) -> p k n", k=2)

        opening_banks = [misc, pv, turned[0], turned[1], scores[:, 0, 0:HALF], scores[:, 0, HALF:N]]

        first_in, weights_in, late_in = sem("first_in"), sem("weights_in"), sem("late_in")
        adj_in = [sem(f"adj_in{i}") for i in range(2)]
        xT_in, x_in = sem("xT_in"), sem("x_in")
        q_stacked = [sem(f"q_stacked{h}") for h in range(HG)]
        k_stacked = [sem(f"k_stacked{h}") for h in range(HG)]
        x1_out = sem("x1_out")
        mask_made, deg_made, guard_step = sem("mask_made"), sem("deg_made"), sem("guard_step")
        bias_made, half_made = sem("bias_made"), sem("half_made")
        scored, lowered, probs_made = sem("scored"), sem("lowered"), sem("probs_made")
        turned_made = [sem(f"turned_made{j}") for j in range(2)]
        turned_kept = [sem(f"turned_kept{j}") for j in range(2)]
        pv_made, attn_made = sem("pv_made"), sem("attn_made")
        recip_made, cols_made, recipT_made, recipT_kept = sem("recip_made"), sem("cols_made"), sem("recipT_made"), sem("recipT_kept")
        qk_made, qk_kept, hi_made, lo_made = sem("qk_made"), sem("qk_kept"), sem("hi_made"), sem("lo_made")
        v_made, v_kept = sem("v_made"), sem("v_kept")
        dve_waited, sp_waited = sem("dve_waited"), sem("sp_waited")

        w_in, adjT_in, edges_made, deg_bias_made = sem("w_in"), [sem(f"adjT_in{t}") for t in range(6)], sem("edges_made"), sem("deg_bias_made")
        x1_in = [sem(f"x1_in{k}") for k in range(2)]
        out_sent = [sem(f"out_sent{k}") for k in range(2)]
        x1_biased, x1_turned, x1T_kept = sem("x1_biased"), sem("x1_turned"), sem("x1T_kept")
        mlp_made, msg_hi_made, msg_lo_made, own_made = sem("mlp_made"), sem("msg_hi_made"), sem("msg_lo_made"), sem("own_made")
        agg_made, half_added, agg_kept = sem("agg_made"), sem("half_added"), sem("agg_kept")
        stats2_made, moments2_made, eps2_made, rstd2_made, normed2 = sem("stats2_made"), sem("moments2_made"), sem("eps2_made"), sem("rstd2_made"), sem("normed2")
        wo_made, wo_kept, x_biased = sem("wo_made"), sem("wo_kept"), sem("x_biased")
        stats_made, moments_made, eps_made, rstd_made, normed = sem("stats_made"), sem("moments_made"), sem("eps_made"), sem("rstd_made"), sem("normed")

        def kept(kind, i, b, g):
            if kind == "r":
                return recipT_kept, queries_before(b, g, i) + 1
            if kind == "wo":
                return wo_kept, (b - 1) * 4 + (i + 1)
            seg = b * G + (g + 1)
            return (qk_kept, seg * 4 + (i + 1)) if i < 4 else (v_kept, seg * 2 + (i - 3))

        def segments(eng, segment):
            for g in range(G):
                segment(0, g, True, False, False)
            with eng.Fori(1, NB - 1) as b:
                for g in range(G):
                    segment(b, g, False, False, False)
            for g in range(G):
                segment(NB - 1, g, False, True, False)
            segment(NB, 0, False, False, True)

        def batches(eng, batch):
            for k in range(2):
                batch(k, k, k == 0, False)
            with eng.Fori(1, NB // 2 - 1) as pair:
                for k in range(2):
                    batch(pair * 2 + k, k, False, False)
            for k in range(2):
                batch(NB - 2 + k, k, False, k == 1)

        block = ctx.enter_context(nc.Block())

        @block.sync
        def _(sp):
            sp.sem_inc(x1_out, 16)
            def load_weight(w, w_dram, landed):
                sp.dma_start(w[:, :, :], w_dram.rearrange("(c p) n -> p c n", p=P)).then_inc(landed, 16)

            load_weight(wq_sb, wqT, first_in)
            sp.dma_start(xT_sb[:, :, :], xT[0].rearrange("(c p) n -> p c n", p=P)).then_inc(xT_in, 16)
            for b_sb, b_dram in ((bq_sb, bq), (bk_sb, bk)):
                sp.dma_start(b_sb[:, :], b_dram).then_inc(first_in, 16)
            load_weight(wk_sb, wkT, first_in)
            load_weight(wv_sb, wvT, weights_in)
            sp.dma_start(bv_sb[:, :], bv.rearrange("(a n) -> a n", a=1).broadcast_to([P, D])).then_inc(weights_in, 16)
            sp.dma_start(ident[:, :], ident_in).then_inc(weights_in, 16)

            def load_adj(t):
                if t >= 2:
                    sp.wait_ge(mask_made, t - 1)
                    sp.wait_ge(deg_made, t - 1)
                sp.dma_start(y_int[:, t % 2, :], adj[t * P:(t + 1) * P, :]).then_inc(adj_in[t % 2], 16)

            load_adj(0)
            load_adj(1)
            load_weight(wo_sb, woT, late_in)
            for b_sb, b_dram in ((bo_sb, bo), (bias_sb, bias)):
                sp.dma_start(b_sb[:, :], b_dram.rearrange("(a n) -> a n", a=1).broadcast_to([P, D])).then_inc(late_in, 16)

            def stack(seg, g, free):
                for parts, dst, landed, i in (((q_hi, q_lo, q_hi, q_lo), q_stack[g], q_stacked, 2),
                                              ((k_hi, k_hi, k_lo, k_lo), k_stack[g], k_stacked, 4)):
                    sp.wait_ge(lo_made, seg * 4 + i)
                    sp.sem_inc(sp_waited, 1)
                    if free is not None:
                        sp.wait_ge(scored, free)
                    for h in range(HG):
                        for j, part in enumerate(parts):
                            sp.dma_start(dst[j * DH:(j + 1) * DH, h, :].bitcast(F32), part[h * DH:(h + 1) * DH, :].bitcast(F32)).then_inc(landed[h], 16)

            stack(0, 0, None)

            def segment(b, g, first, last, drain):
                if g == 0 and not drain:
                    if not first:
                        sp.wait_ge(wo_kept, b * 4)
                    sp.sem_inc(sp_waited, 1)
                    sp.dma_start(x_sb[:, :, :], x[b].rearrange("(t p) d -> p t d", p=P)).then_inc(x_in, 16)
                    for t in range(2, NT if first else 2):
                        load_adj(t)
                if not (last and g == 1) and not drain:
                    stack(b * G + (g + 1), 1 - g, None if first and g == 0 else units_before(b, g, 0))
                if g == 0 and last:
                    sp.wait_ge(v_made, (b * G + 2) * 2)
                    sp.wait_ge(lo_made, (b * G + 2) * 4)
                    sp.dma_start(w_sb[:, :, :], wijT.rearrange("(c p) n -> p c n", p=P)).then_inc(w_in, 16)
                    for t in range(2):
                        sp.dma_start(edges_int[t], adjT[t * P:(t + 1) * P, :]).then_inc(adjT_in[t], 16)
                if g == 0 and not last and not drain:
                    sp.wait_ge(v_made, (b * G + 2) * 2)
                    sp.sem_inc(sp_waited, 1)
                    sp.wait_ge(qk_made, (b * G + 2) * 4)
                    sp.sem_inc(sp_waited, 1)
                    sp.dma_start(xT_sb[:, :, :], xT[b + 1].rearrange("(c p) n -> p c n", p=P)).then_inc(xT_in, 16)
                if g == 0 and not first and not drain:
                    sp.wait_ge(normed, b * NT)
                    sp.sem_inc(sp_waited, 1)
                    sp.dma_start(x1[b - 1].rearrange("(t p) d -> p t d", p=P), y_sb[:, :, :]).then_inc(x1_out, 16)

            segments(sp, segment)

            def load_edges(t, place):
                sp.dma_start(edges_int[place], adjT[t * P:(t + 1) * P, :]).then_inc(adjT_in[place], 16)

            sp.wait_ge(turned_made[1], NB * G * UNITS)
            sp.wait_ge(lowered, NB * G * UNITS)
            sp.dma_start(x1_sb[:, 0, :, :], x1[0].rearrange("(t p) d -> p t d", p=P)).then_inc(x1_in[0], 16)
            for t in range(2, 6):
                load_edges(t, t)
            def batch(b, k, first, last):
                if not last:
                    if not first:
                        sp.wait_ge(own_made, b * NT)
                        sp.sem_inc(sp_waited, 1)
                    sp.dma_start(x1_sb[:, 1 - k, :, :], x1[b + 1].rearrange("(t p) d -> p t d", p=P)).then_inc(x1_in[1 - k], 16)
                if first:
                    for t in range(2):
                        sp.wait_ge(edges_made, t + 1)
                        load_edges(6 + t, t)
                    sp.wait_ge(normed, NB * NT)
                    sp.dma_start(x1[NB - 1].rearrange("(t p) d -> p t d", p=P), y_sb[:, :, :]).then_inc(x1_out, 16)
                sp.wait_ge(normed2, b * NT + NT)
                sp.sem_inc(sp_waited, 1)
                sp.dma_start(out[b].rearrange("(t p) d -> p t d", p=P), out_sb[k][:, :, :]).then_inc(out_sent[k], 16)
                if first:
                    sp.wait_ge(x1_out, (NB + 1) * 16)

            batches(sp, batch)
            for k in range(2):
                sp.wait_ge(out_sent[k], NB // 2 * 16)

        @block.gpsimd
        def _(pool):
            pool.memset(neg_half[:, :], -0.5).then_inc(half_made, 1)
            pool.wait_ge(half_made, 1)
            pool.wait_ge(late_in, 3 * 16)

            def batch(b):
                pool.wait_ge(x_in, b * 16 + 16)
                pool.tensor_tensor(x_sb[:, :, :], x_sb[:, :, :], bo_sb[:, :].unsqueeze(1).broadcast_to([P, NT, D]),
                                   ALU.add).then_inc(x_biased, 1)
                pool.wait_ge(eps_made, b + 1)
                pool.tensor_tensor(rstd[:, :], var_eps[:, :], neg_half[:, :], ALU.pow).then_inc(rstd_made, 1)

            with pool.Fori(0, NB) as b:
                batch(b)

            def convolve(b, k, first, last):
                for t in range(NT):
                    pool.wait_ge(eps2_made, b * NT + (t + 1))
                    nc.gpsimd.tensor_tensor(rstd[:, t:t + 1], var_eps[:, t:t + 1], neg_half[:, t:t + 1], ALU.pow).then_inc(rstd2_made, 1)

            pool.wait_ge(normed, NB * NT)
            batches(pool, convolve)

        @block.scalar
        def _(act):
            act.wait_ge(bias_made, 2)

            def project(seg, i, reused):
                kind, half = PIECES[i]
                act.wait_ge(qk_made, seg * 4 + (i + 1))
                if reused or i >= 2:
                    act.wait_ge(lo_made, seg * 4 + (i - 1))
                hi, bias, scale, landed = (q_hi, bq_c, SCALE, q_stacked) if kind == "q" else (k_hi, bk_c, -1.0, k_stacked)
                gg = project.group
                bank = misc if reused else opening_banks[i]
                act.activation(full[:, half, :], bank[:, :], ACT.Identity, bias=bias[:, gg:gg + 1], scale=scale).then_inc(qk_kept, 1)
                act.wait_ge(qk_kept, seg * 4 + (i + 1))
                if reused and half == 0:
                    for h in range(HG):
                        act.wait_ge(landed[h], seg * (STACKS * 16))
                act.activation(hi[:, half * HALF:(half + 1) * HALF], full[:, half, :], ACT.Copy).then_inc(hi_made, 1)

            project.group = 0
            def degree(t):
                act.wait_ge(adj_in[t % 2], (t // 2 + 1) * 16)
                if t > 0:
                    act.wait_ge(deg_made, t)
                act.activation(scratch[:, :], y_int[:, t % 2, :], ACT.Copy, accum_out=deg[:, t:t + 1]).then_inc(deg_made, 1)

            for i in range(4):
                project(0, i, False)
            degree(0)
            degree(1)

            def segment(b, g, first, last, drain):
                pre_steps = {} if drain or (last and g == 1) else {u + 1: i for i, u in enumerate(PIECE_STEPS) if i < 4}
                opening = first and g == 0
                for u in range(LAG + 5 if drain else UNITS):
                    t = u - LAG
                    if not (opening and t < 0) and not (drain and t >= 0):
                        act.wait_ge(turned_made[0], units_before(b, g, t) + 1)
                        if t % HG == 0 and not (opening and t < 2 * HG):
                            act.wait_ge(pv_made, queries_before(b, g, t // HG - 1))
                        act.activation(probsT[:, t // HG % 2, t % HG, 0:HALF], turned[0][:, :], ACT.Copy).then_inc(turned_kept[0], 1)
                        if t % HG in ACT_BOTH:
                            act.wait_ge(turned_made[1], units_before(b, g, t) + 1)
                            act.activation(probsT[:, t // HG % 2, t % HG, HALF:N], turned[1][:, :], ACT.Copy).then_inc(turned_kept[1], 1)
                    q = (u - 7) // HG
                    if u % HG == 3 and not (opening and q < 0) and not (drain and q >= 0):
                        act.wait_ge(recipT_made, queries_before(b, g, q) + 1)
                        if not (opening and q < 1):
                            act.wait_ge(attn_made, queries_before(b, g, q))
                        act.activation(recipT[:, :], misc[:, 0:P], ACT.Copy).then_inc(recipT_kept, 1)
                    if u in pre_steps:
                        project.group = 1 - g
                        project(b * G + (g + 1), pre_steps[u], True)
                    if (u == 0 or not drain) and not (opening and u == 0):
                        e = u - 1
                        act.wait_ge(lowered, units_before(b, g, u))
                        act.activation(ring[:, e % RING, :], ring[:, e % RING, :], ACT.Exp, bias=low[:, e % RING:e % RING + 1],
                                       scale=-1.0, accum_out=sums[:, e // HG % 2, e % HG:e % HG + 1]).then_inc(probs_made, 1)
                    if opening and u % HG == 1 and u // HG + 2 < NT:
                        degree(u // HG + 2)

            segments(act, segment)

            def keep_turned(batch_no, i):
                act.wait_ge(x1_turned, batch_no * 4 + (i + 1))
                nc.scalar.activation(x1T[:, :, 2 * i * P:(2 * i + 2) * P], turned[i % 2][:, :].rearrange("p (c n) -> p c n", c=DC),
                                     ACT.Copy).then_inc(x1T_kept, 1)

            act.wait_ge(scored, NB * G * UNITS)
            for i in range(4):
                keep_turned(0, i)

            def batch(b, k, first, last):
                for t in range(NT):
                    act.wait_ge(mlp_made, b * NT + (t + 1))
                    if t == 0 and not first:
                        act.wait_ge(agg_made, b * NT)
                    nc.scalar.activation(msg[:, t, 0:D], mlp[:, t % 2, D:2 * D], ACT.Copy).then_inc(msg_hi_made, 1)
                    if first:
                        act.wait_ge(adjT_in[t % 6], t // 6 * 16 + 16)
                        nc.scalar.activation(edges[t], edges_int[t % 6], ACT.Copy).then_inc(edges_made, 1)
                if not last:
                    for i in range(4):
                        keep_turned(b + 1, i)

            batches(act, batch)

        @block.vector
        def _(dve):
            dve.wait_ge(first_in, 4 * 16)
            nc.vector.tensor_scalar(bq_c[:, :], bq_sb[:, :], SCALE, None, ALU.mult).then_inc(bias_made, 1)
            nc.vector.tensor_scalar(bk_c[:, :], bk_sb[:, :], -1.0, None, ALU.mult).then_inc(bias_made, 1)

            def low_part(seg, i, reused):
                kind, half = PIECES[i]
                hi, lo, landed = (q_hi, q_lo, q_stacked) if kind == "q" else (k_hi, k_lo, k_stacked)
                cols = slice(half * HALF, (half + 1) * HALF)
                dve.wait_ge(hi_made, seg * 4 + (i + 1))
                if reused and half == 0:
                    for h in range(HG):
                        dve.wait_ge(landed[h], seg * (STACKS * 16))
                nc.vector.tensor_tensor(lo[:, cols], full[:, half, :], hi[:, cols].bitcast(F32), ALU.subtract).then_inc(lo_made, 1)

            def keep_v(seg, g, i, free):
                dve.wait_ge(v_made, seg * 2 + (i + 1))
                if free is None and seg == 0:
                    dve.wait_ge(weights_in, 3 * 16)
                if free is not None:
                    dve.wait_ge(pv_made, free)
                bank = opening_banks[4 + i] if free is None and isinstance(seg, int) and seg == 0 else misc
                nc.vector.tensor_tensor(v_rows[g][:, 4 * i:4 * i + 4, :], bank[:, :].rearrange("p (t n) -> p t n", t=4),
                                        bv_sb[:, g * P:(g + 1) * P].unsqueeze(1).broadcast_to([P, 4, P]), ALU.add).then_inc(v_kept, 1)

            def make_mask(t):
                dve.wait_ge(adj_in[t % 2], (t // 2 + 1) * 16)
                nc.vector.tensor_scalar(mask[:, t, :], y_int[:, t % 2, :], 0, MASKED, ALU.is_equal, ALU.mult).then_inc(mask_made, 1)

            def make_guard(t):
                row = slice(t, t + 1)
                dve.wait_ge(mask_made, t + 1)
                nc.vector.tensor_reduce(row_low[:, row], mask[:, t, :], AXX, ALU.min).then_inc(guard_step, 1)
                dve.wait_ge(guard_step, 4 * t + 1)
                nc.vector.tensor_scalar(has_edge[:, row], row_low[:, row], 0.0, None, ALU.is_equal).then_inc(guard_step, 1)
                dve.wait_ge(guard_step, 4 * t + 2)
                nc.vector.reciprocal(has_inv[:, row], has_edge[:, row]).then_inc(guard_step, 1)
                dve.wait_ge(guard_step, 4 * t + 3)
                nc.vector.tensor_tensor(guard[:, row], has_edge[:, row], has_inv[:, row], ALU.mult).then_inc(guard_step, 1)

            for i in range(4):
                low_part(0, i, False)
            for i in range(2):
                keep_v(0, 0, i, None)
            make_mask(0)
            make_mask(1)

            def normalise(t):
                nc.vector.tensor_scalar(y_sb[:, t, :], y_sb[:, t, :], moments[:, t, 0:1], rstd[:, t:t + 1],
                                        ALU.subtract, ALU.mult).then_inc(normed, 1)

            def segment(b, g, first, last, drain):
                opening = first and g == 0
                pre = not drain and not (last and g == 1)
                pre_steps = {u + 1: i for i, u in enumerate(PIECE_STEPS)} if pre else {}
                wo_steps = {u + 1: p for p, u in enumerate(WO_STEPS)} if g == 0 and not first else {}
                post = g == 0 and not first
                for u in range(DRAIN if drain else UNITS):
                    q = (u - 11) // HG
                    if u % HG == 3 and not (opening and q < 0) and not (drain and q >= 0):
                        gq = g if q >= 0 else 1 - g
                        t = q % NT
                        dve.wait_ge(pv_made, queries_before(b, g, q) + 1)
                        dve.wait_ge(recipT_kept, queries_before(b, g, q) + 1)
                        if not first and q >= 0:
                            dve.wait_ge(wo_made, (b - 1) * 4 + (t // 2 + 1))
                        nc.vector.tensor_tensor(attnT[:, gq, t * P:(t + 1) * P], pv[:, 0:P], recipT[:, :], ALU.mult).then_inc(attn_made, 1)
                    if post and STAT_STEP < u <= STAT_STEP + NT:
                        dve.wait_ge(stats_made, (b - 1) * NT + (u - STAT_STEP))
                    e = u - 1
                    if (u == 0 or not drain) and not (opening and u == 0):
                        dve.wait_ge(scored, units_before(b, g, e) + 1)
                        if not (opening and e < RING):
                            dve.wait_ge(turned_made[1], units_before(b, g, e) - (RING - 1))
                        if opening and e % HG == 0:
                            dve.wait_ge(mask_made, e // HG + 1)
                        dve.sem_inc(dve_waited, 1)
                        nc.vector.tensor_tensor_reduce(ring[:, e % RING, :], scores[:, e % 2, :], mask[:, e // HG % NT, :], 1.0, 3e38,
                                                       ALU.add, ALU.min, low[:, e % RING:e % RING + 1]).then_inc(lowered, 1)
                    t = u - LAG
                    if t % HG not in ACT_BOTH and not (opening and t < 0) and not (drain and t >= 0):
                        dve.wait_ge(turned_made[1], units_before(b, g, t) + 1)
                        if t % HG == 0 and not (opening and t < 2 * HG):
                            dve.wait_ge(pv_made, queries_before(b, g, t // HG - 1))
                        nc.vector.tensor_copy(probsT[:, t // HG % 2, t % HG, HALF:N], turned[1][:, :]).then_inc(turned_kept[1], 1)
                    if opening and u % HG == 1 and u // HG + 2 < NT:
                        make_mask(u // HG + 2)
                    if opening and u % HG == 2:
                        make_guard(u // HG)
                        if u // HG == NT - 1:
                            dve.wait_ge(guard_step, 4 * NT)
                    q = (u - 5) // HG
                    if u % HG == 1 and not (opening and q < 0) and not (drain and q >= 0):
                        t = q % NT
                        dve.wait_ge(probs_made, units_before(b, g, HG * q + HG))
                        nc.vector.reciprocal(recip[:, :], sums[:, q % 2, :]).then_inc(recip_made, 1)
                        dve.wait_ge(recip_made, queries_before(b, g, q) + 1)
                        if not (opening and q < 1):
                            dve.wait_ge(recipT_made, queries_before(b, g, q))
                        if opening:
                            dve.wait_ge(guard_step, 4 * t + 4)
                        nc.vector.tensor_scalar(recip_cols[:, :, :], recip[:, :].unsqueeze(2).broadcast_to([P, HG, DH]),
                                                guard[:, t:t + 1], None, ALU.mult).then_inc(cols_made, 1)
                    if u in pre_steps:
                        i = pre_steps[u]
                        if i < 4:
                            low_part(b * G + (g + 1), i, True)
                        else:
                            keep_v(b * G + (g + 1), 1 - g, i - 4, None if opening else queries_before(b, g, 0))
                    if u in wo_steps:
                        p = wo_steps[u]
                        dve.wait_ge(wo_made, (b - 1) * 4 + (p + 1))
                        if p == 0:
                            dve.wait_ge(x_biased, b)
                            dve.wait_ge(x1_out, b * 16)
                        nc.vector.tensor_tensor(y_sb[:, 2 * p:2 * p + 2, :], misc[:, :].rearrange("p (t n) -> p t n", t=2),
                                                x_sb[:, 2 * p:2 * p + 2, :], ALU.add).then_inc(wo_kept, 1)
                    if post and STAT_STEP <= u < STAT_STEP + NT:
                        t = u - STAT_STEP
                        dve.wait_ge(wo_kept, (b - 1) * 4 + (t // 2 + 1))
                        nc.vector.bn_stats(stats[:, t, :], y_sb[:, t, :]).then_inc(stats_made, 1)
                    if post and STAT_STEP < u <= STAT_STEP + NT:
                        t = u - STAT_STEP - 1
                        nc.vector.bn_aggr(moments[:, t, :], stats[:, t, :]).then_inc(moments_made, 1)
                    if post and u == EPS_STEP:
                        dve.wait_ge(moments_made, b * NT)
                        nc.vector.tensor_scalar(var_eps[:, :], moments[:, :, 1], EPS, None, ALU.add).then_inc(eps_made, 1)
                    if post and not drain and NORM_STEP <= u < NORM_STEP + NT:
                        dve.wait_ge(rstd_made, b)
                        normalise(u - NORM_STEP)

            segments(dve, segment)

            dve.wait_ge(late_in, 3 * 16)
            dve.wait_ge(wo_kept, NB * 4)
            dve.wait_ge(rstd_made, NB)
            dve.wait_ge(pv_made, NB * G * NT)

            def norm(b, k, t):
                dve.wait_ge(rstd2_made, b * NT + (t + 1))
                nc.vector.tensor_scalar(out_sb[k][:, t, :], out_sb[k][:, t, :], moments[:, t, 0:1], rstd[:, t:t + 1],
                                        ALU.subtract, ALU.mult).then_inc(normed2, 1)

            def moments_of(b, t):
                nc.vector.bn_aggr(moments[:, t, :], stats[:, t, :]).then_inc(moments2_made, 1)

            def eps_of(b, t):
                dve.wait_ge(moments2_made, b * NT + (t + 1))
                nc.vector.tensor_scalar(var_eps[:, t:t + 1], moments[:, t, 1:2], EPS, None, ALU.add).then_inc(eps2_made, 1)

            def batch(b, k, first, last):
                dve.wait_ge(x1_in[k], (b - k) * 8 + 16)
                for t in range(NT):
                    if first:
                        nc.vector.tensor_scalar(deg_bias[:, t, :], bias_sb[:, :], deg[:, t:t + 1], None, ALU.mult).then_inc(deg_bias_made, 1)
                        dve.wait_ge(deg_bias_made, t + 1)
                    nc.vector.tensor_tensor(x1_bias[:, t, :], x1_sb[:, k, t, :], deg_bias[:, t, :], ALU.add).then_inc(x1_biased, 1)
                    dve.wait_ge(msg_hi_made, b * NT + (t + 1))
                    nc.vector.tensor_tensor(msg[:, t, D:2 * D], mlp[:, t % 2, D:2 * D], msg[:, t, 0:D].bitcast(F32),
                                            ALU.subtract).then_inc(msg_lo_made, 1)
                    dve.wait_ge(x1_biased, b * NT + (t + 1))
                    nc.vector.scalar_tensor_tensor(out=own[:, t, :], in0=mlp[:, t % 2, 0:D], scalar=deg[:, t:t + 1],
                                                   in1=x1_bias[:, t, :], op0=ALU.mult, op1=ALU.add).then_inc(own_made, 1)
                    if first:
                        normalise(t)
                    elif t < 3:
                        norm(b - 1, 1 - k, NT - 3 + t)

                dve.wait_ge(own_made, b * NT + NT)
                if not (isinstance(b, int) and b < 2):
                    dve.wait_ge(out_sent[k], (b - k) * 8)
                for t in range(NT):
                    done = b * NT + (t + 1)
                    dve.wait_ge(agg_made, done)
                    nc.vector.tensor_tensor(out_sb[k][:, t, :], agg[:, t % 2, 0:D], own[:, t, :], ALU.add).then_inc(half_added, 1)
                    if t >= 3:
                        norm(b, k, t - 3)
                    if t > 0:
                        dve.wait_ge(stats2_made, done - 1)
                    dve.wait_ge(half_added, done)
                    nc.vector.tensor_tensor(out_sb[k][:, t, :], agg[:, t % 2, D:2 * D], out_sb[k][:, t, :], ALU.add).then_inc(agg_kept, 1)
                    if t > 0:
                        moments_of(b, t - 1)
                    dve.wait_ge(agg_kept, done)
                    nc.vector.bn_stats(stats[:, t, :], out_sb[k][:, t, :]).then_inc(stats2_made, 1)
                    if t > 0:
                        eps_of(b, t - 1)
                dve.wait_ge(stats2_made, b * NT + NT)
                dve.sem_inc(dve_waited, 1)
                moments_of(b, NT - 1)
                eps_of(b, NT - 1)

            batches(dve, batch)
            for t in range(NT - 3, NT):
                norm(NB - 1, 1, t)

        @block.tensor
        def _(pe):
            pe.wait_ge(first_in, 4 * 16)
            pe.wait_ge(xT_in, 16)

            def project(seg, g, i, dst):
                kind, half = PIECES[i]
                if kind == "v":
                    for t in range(4):
                        rows = slice((4 * half + t) * P, (4 * half + t + 1) * P)
                        for c in range(DC):
                            last = nc.tensor.matmul(dst[:, t * P:(t + 1) * P], xT_sb[:, c, rows], wv_sb[:, c, g * P:(g + 1) * P],
                                                    start=(c == 0), stop=(c == DC - 1))
                    last.then_inc(v_made, 1)
                else:
                    w = wq_sb if kind == "q" else wk_sb
                    for c in range(DC):
                        last = nc.tensor.matmul(dst[:, :], w[:, c, g * P:(g + 1) * P], xT_sb[:, c, half * HALF:(half + 1) * HALF],
                                                start=(c == 0), stop=(c == DC - 1))
                    last.then_inc(qk_made, 1)

            for i in range(len(PIECES)):
                if i == 4:
                    pe.wait_ge(weights_in, 3 * 16)
                project(0, 0, i, opening_banks[i])
            pe.wait_ge(qk_kept, 4)
            pe.wait_ge(v_kept, 2)

            def segment(b, g, first, last, drain):
                opening = first and g == 0
                users = misc_users(g, first, last, drain)
                for u in range(LAG + 8 if drain else UNITS):
                    t = u - LAG
                    turn = not (opening and t < 0) and not (drain and t >= 0)
                    for j in range(2):
                        if turn:
                            if j == 0:
                                pe.wait_ge(probs_made, units_before(b, g, t) + 1)
                            if not (opening and t < 1):
                                pe.wait_ge(turned_kept[j], units_before(b, g, t))
                            for c in range(4):
                                k = 4 * j + c
                                mm = nc.tensor.transpose(turned[j][:, c * P:(c + 1) * P], ring[:, t % RING, k * P:(k + 1) * P], ident[:, :])
                            mm.then_inc(turned_made[j], 1)
                        if not drain:
                            if j == 0:
                                if not (opening and u < 2):
                                    pe.wait_ge(lowered, units_before(b, g, u) - 1)
                                if u < HG:
                                    pe.wait_ge(q_stacked[u], (b * G + (g + 1)) * (STACKS * 16))
                                    pe.wait_ge(k_stacked[u], (b * G + (g + 1)) * (STACKS * 16))
                            h, q = u % HG, u // HG
                            mm = nc.tensor.matmul(scores[:, u % 2, j * HALF:(j + 1) * HALF], q_stack[g][:, h, q * P:(q + 1) * P],
                                                  k_stack[g][:, h, j * HALF:(j + 1) * HALF], start=True, stop=True)
                            if j == 1:
                                mm.then_inc(scored, 1)
                    q, c = (u - 7) // HG, (u - 7) % HG
                    if not (opening and q < 0) and not (drain and q >= 0):
                        gq = g if q >= 0 else 1 - g
                        if c == 0:
                            for j in range(2):
                                pe.wait_ge(turned_kept[j], units_before(b, g, HG * q + HG))
                            if not (opening and q < 1):
                                pe.wait_ge(attn_made, queries_before(b, g, q))
                            if q == 0:
                                pe.wait_ge(v_kept, (b * G + (g + 1)) * 2)
                        for k in (2 * c, 2 * c + 1):
                            for h in range(HG):
                                mm = nc.tensor.matmul(pv[h * DH:(h + 1) * DH, 0:P], v_rows[gq][:, k, h * DH:(h + 1) * DH],
                                                      probsT[:, q % 2, h, k * P:(k + 1) * P], start=(k == 0), stop=(k == NT - 1))
                        if c == HG - 1:
                            mm.then_inc(pv_made, 1)
                    for n, (at, kind, i) in enumerate(users):
                        if at != u:
                            continue
                        if n > 0:
                            pe.wait_ge(*kept(*users[n - 1][1:], b, g))
                        elif not opening:
                            pe.wait_ge(recipT_kept, queries_before(b, g, i))
                        if kind == "r":
                            pe.wait_ge(cols_made, queries_before(b, g, i) + 1)
                            nc.tensor.transpose(misc[:, 0:P], recip_cols[:, :, :].rearrange("p h d -> p (h d)"), ident[:, :]).then_inc(recipT_made, 1)
                        elif kind == "wo":
                            pe.wait_ge(late_in, 3 * 16)
                            pe.wait_ge(attn_made, queries_before(b - 1, 1, 2 * i + 2))
                            for j in range(2):
                                rows = slice((2 * i + j) * P, (2 * i + j + 1) * P)
                                for c in range(G):
                                    mm = nc.tensor.matmul(misc[:, j * D:(j + 1) * D], attnT[:, c, rows], wo_sb[:, c, :],
                                                          start=(c == 0), stop=(c == G - 1))
                            mm.then_inc(wo_made, 1)
                        else:
                            if g == 1 and i == 0:
                                pe.wait_ge(xT_in, b * 16 + 32)
                            project(b * G + (g + 1), 1 - g, i, misc)

            segments(pe, segment)

            def turn(batch_no, k, i, opening):
                if i == 0:
                    pe.wait_ge(x1_in[k], (batch_no - k) * 8 + 16)
                if not (opening and i < 2):
                    pe.wait_ge(x1T_kept, batch_no * 4 + (i - 1))
                for j in range(2):
                    for c in range(DC):
                        mm = nc.tensor.transpose(turned[i % 2][:, c * D + j * P:c * D + (j + 1) * P],
                                                 x1_sb[:, k, 2 * i + j, c * P:(c + 1) * P], ident[:, :])
                mm.then_inc(x1_turned, 1)

            for j in range(2):
                pe.wait_ge(turned_kept[j], NB * G * UNITS)
            for i in range(4):
                turn(0, 0, i, True)
            pe.wait_ge(w_in, 16)
            pe.wait_ge(lowered, NB * G * UNITS)

            def batch(b, k, first, last):
                for t in range(NT):
                    if t % 2 == 0:
                        pe.wait_ge(x1T_kept, b * 4 + (t // 2 + 1))
                    if t >= 2:
                        pe.wait_ge(own_made, b * NT + (t - 1))
                    elif not first:
                        pe.wait_ge(own_made, b * NT)
                    for c in range(DC):
                        mm = nc.tensor.matmul(mlp[:, t % 2, :], x1T[:, c, t * P:(t + 1) * P], w_sb[:, c, :],
                                              start=(c == 0), stop=(c == DC - 1))
                    mm.then_inc(mlp_made, 1)
                if not last:
                    turn(b + 1, 1 - k, 0, False)
                    turn(b + 1, 1 - k, 1, False)
                if first:
                    pe.wait_ge(edges_made, NT)
                pe.wait_ge(msg_lo_made, b * NT + NT)
                for t in range(NT):
                    if t >= 2:
                        pe.wait_ge(agg_kept, b * NT + (t - 1))
                    elif not first:
                        pe.wait_ge(agg_kept, b * NT)
                    for j in range(NT):
                        mm = nc.tensor.matmul(agg[:, t % 2, :], edges[j][:, t * P:(t + 1) * P], msg[:, j, :],
                                              start=(j == 0), stop=(j == NT - 1))
                    mm.then_inc(agg_made, 1)
                    if t in (1, 3) and not last:
                        turn(b + 1, 1 - k, (t + 3) // 2, False)

            batches(pe, batch)


def kernel(x, adj, L0_gnn_Wq, L0_gnn_bq, L0_gnn_Wk, L0_gnn_bk, L0_gnn_Wv, L0_gnn_bv, L0_gnn_Wo, L0_gnn_bo, L1_gnn_W, L1_gnn_b):
    import numpy as np
    import concourse.bacc as bacc
    from concourse.bass_utils import run_bass_kernel_spmd

    def laid(a):
        return np.ascontiguousarray(a)

    x, adj, w1 = np.asarray(x), np.asarray(adj), np.asarray(L1_gnn_W)
    arrays = {
        "x": laid(x), "xT": laid(x.transpose(0, 2, 1)), "adj": laid(adj), "adjT": laid(adj.T),
        "ident": np.eye(P, dtype=np.float32),
        "wqT": laid(np.asarray(L0_gnn_Wq).T), "bq": laid(np.asarray(L0_gnn_bq).reshape(G, P).T), "wkT": laid(np.asarray(L0_gnn_Wk).T), "bk": laid(np.asarray(L0_gnn_bk).reshape(G, P).T),
        "wvT": laid(np.asarray(L0_gnn_Wv).T), "bv": laid(L0_gnn_bv), "woT": laid(np.asarray(L0_gnn_Wo).T), "bo": laid(L0_gnn_bo),
        "wijT": laid(w1.reshape(D, 2, D).transpose(2, 1, 0).reshape(D, 2 * D)), "bias": laid(L1_gnn_b),
    }
    nc = bacc.Bacc("TRN2", target_bir_lowering=False, num_devices=1)
    args = [nc.dram_tensor(n + "_dram", a.shape, mybir.dt.from_np(a.dtype), kind="ExternalInput").ap() for n, a in arrays.items()]
    out = nc.dram_tensor("out_dram", x.shape, F32, kind="ExternalOutput").ap()
    x1 = nc.dram_tensor("x1_dram", x.shape, F32, kind="Internal").ap()
    gnn_layers(nc, *args, x1, out)
    r = run_bass_kernel_spmd(nc, [{n + "_dram": a for n, a in arrays.items()}], core_ids=[0])
    return r.results[0]["out_dram"]
```

```python
from contextlib import ExitStack

import concourse.bass as bass
from concourse import mybir

F32 = mybir.dt.float32
F32R = mybir.dt.float32r
BF16 = mybir.dt.bfloat16
I32 = mybir.dt.int32
ALU = mybir.AluOpType
ACT = mybir.ActivationFunctionType
AXX = mybir.AxisListType.X

P = 128
NB, N, D = 8, 1024, 256
H, DH = 8, 32
HG = P // DH
G = H // HG
NT = N // P
DC = D // P
HALF = 512
UNITS = HG * NT
PAIR = 2 * HG
LAG = 3
ACT_BOTH = (1, 2, 4, 7)
LAST_PARTS = 4
RING = 4
MASKED = -1e30
EPS = 1e-5
SCALE = 1.0 / DH ** 0.5
STACKS = P // DH
PIECES = (("q", 0), ("q", 1), ("k", 0), ("k", 1), ("v", 0), ("v", 1))
PIECE_STEPS = ((8, 10, 16, 18, 20, 26), (8, 10, 16, 18, 24, 26))
WO_STEPS = (0, 2, 4, 12)
STAT_STEP, EPS_STEP, NORM_STEP = 8, 17, 19
PV_STEP = LAG + PAIR
FIRST_KEY_PART = 1
RECIP_STEP = 13
ATTN_STEP = 18
DRAIN = EPS_STEP + 1


def units_before(b, g, u):
    return b * (G * UNITS) + (g * UNITS + u)


def pairs_before(b, g, p):
    return b * (G * NT // 2) + (g * NT // 2 + p)


def misc_users(g, first, last, drain):
    users = [(RECIP_STEP + 1 + PAIR * p, "r", p) for p in range(-1, UNITS // PAIR - 1)
             if not (first and g == 0 and p < 0) and not (drain and p >= 0)]
    if g == 0 and not first:
        users += [(u, "wo", p) for p, u in enumerate(WO_STEPS)]
    if not (last and g == 1) and not drain:
        users += [(u, "pre", i) for i, u in enumerate(PIECE_STEPS[g]) if not (first and g == 0 and i >= 4)]
    return sorted(users, key=lambda user: (user[0], user[1] != "r"))


def gnn_layers(nc, x, xT, adj, adjT, ident_in, wqT, bq, wkT, bk, wvT, bv, woT, bo, wijT, bias, x1, out):
    with ExitStack() as ctx:
        def sb(name, shape, dt=F32):
            return ctx.enter_context(nc.sbuf_tensor(name, shape, dt))

        def sem(name):
            return ctx.enter_context(nc.semaphore(name))

        q_stack = [sb(f"q_stack{g}", [P, HG, N], F32R) for g in range(G)]
        k_stack = [sb(f"k_stack{g}", [P, HG, N], F32R) for g in range(G)]
        v_rows = [sb(f"v_rows{g}", [P, NT, P]) for g in range(G)]
        mask = sb("mask", [P, NT, N], BF16)
        ring = sb("ring", [P, RING, N])
        probsT = sb("probsT", [P, PAIR, NT, P])
        attnT = sb("attnT", [P, G, N])
        xT_sb = sb("xT_sb", [P, DC, N])
        x_sb = sb("x_sb", [P, NT, D])
        y_sb = sb("y_sb", [P, NT, D])
        w_sb = sb("w_sb", [P, DC, 2 * D])
        q_hi, q_lo = sb("q_hi", [P, N], F32R), sb("q_lo", [P, N], F32R)
        k_hi, k_lo = sb("k_hi", [P, N], F32R), sb("k_lo", [P, N], F32R)
        wq_sb, wk_sb, wv_sb, wo_sb = (sb(f"w{n}_sb", [P, DC, D]) for n in "qkvo")
        bq_sb, bk_sb = (sb(n, [P, G]) for n in ("bq_sb", "bk_sb"))
        bv_sb, bo_sb, bias_sb = (sb(n, [P, D]) for n in ("bv_sb", "bo_sb", "bias_sb"))
        ident = sb("ident", [P, P])
        scratch = sb("scratch", [P, N], BF16)
        deg = sb("deg", [P, NT])
        low = sb("low", [P, RING])
        sums = sb("sums", [P, 2, PAIR])
        recip = sb("recip", [P, PAIR])
        recip_cols = sb("recip_cols", [P, PAIR, DH])
        recipT = sb("recipT", [P, 2 * P])
        row_high, has_edge, has_inv, guard = (sb(n, [P, NT]) for n in ("row_high", "has_edge", "has_inv", "guard"))
        stats, moments = sb("stats", [P, NT, 6]), sb("moments", [P, NT, 2])
        var_eps, rstd, neg_half = (sb(n, [P, NT]) for n in ("var_eps", "rstd", "neg_half"))
        x_int, y_int = (rows[:, :, :].bitcast(I32).rearrange("p (c t) d -> p c (t d)", c=2) for rows in (x_sb, y_sb))
        adj_sb = [attnT[:, t, :].bitcast(I32) for t in range(2)] + [y_int[:, t, :] for t in range(2)] + [x_int[:, t, :] for t in range(2)]
        adj_sb += adj_sb[2:4]

        scores = ctx.enter_context(nc.psum_tensor("scores", [P, 2, N], F32))
        turned = [ctx.enter_context(nc.psum_tensor(f"turned{j}", [P, HALF], F32)) for j in range(2)]
        pv = ctx.enter_context(nc.psum_tensor("pv", [P, HALF], F32))
        misc = ctx.enter_context(nc.psum_tensor("misc", [P, HALF], F32))

        edges = [k_stack[t // HG][:, t % HG, :] for t in range(NT)]
        edges_int = [xT_sb[:, t, :].bitcast(I32) for t in range(2)] + [ring[:, t, :].bitcast(I32) for t in range(RING)]
        x1_sb = mask[:, :, :].bitcast(F32).rearrange("p (k t) (u d) -> p k (t u) d", k=2, u=2)
        x1T = attnT
        msg = q_stack[0][:, :, :].rearrange("p h (t n) -> p (h t) n", t=2)
        deg_bias = x_sb
        own, x1_bias, out_sb0, out_sb1 = (probsT[:, 2 * k:2 * k + 2, :, :].rearrange("p a (t two) n -> p (a t) (two n)", two=D // P)
                                          for k in range(4))
        out_sb = (out_sb0, out_sb1)
        mlp = scores[:, 0, :].rearrange("p (k n) -> p k n", k=2)
        agg = scores[:, 1, :].rearrange("p (k n) -> p k n", k=2)

        def turned_place(t, half):
            pair, unit, keys = t // PAIR, t % PAIR, slice(half * NT // 2, (half + 1) * NT // 2)
            return probsT[:, unit, keys, :] if pair % 2 == 0 else probsT[:, keys, unit, :]

        def turned_of(pair, h, k):
            return probsT[:, h:PAIR:HG, k, :] if pair % 2 == 0 else probsT[:, k, h:PAIR:HG, :]

        def place_left(b, g, t):
            return pairs_before(b, g, t // PAIR - 1) * NT + (t % PAIR + 1)

        def keep_in_place(eng_copy, h, kind):
            parts, dst, landed = (((q_hi, q_lo, q_hi, q_lo), q_stack[0], q_stacked) if kind == "q" else
                                  ((k_hi, k_hi, k_lo, k_lo), k_stack[0], k_stacked))
            rows = slice(h * DH, (h + 1) * DH)
            eng_copy(dst[rows, h, :], parts[h][rows, :]).then_inc(landed[h], 16)

        opening_banks = [misc, pv, turned[0], turned[1], scores[:, 0, 0:HALF], scores[:, 0, HALF:N]]
        second_v_banks = [scores[:, 1, 0:HALF], scores[:, 1, HALF:N]]

        wq_in, wk_in, bias_in, weights_in, late_in = sem("wq_in"), sem("wk_in"), sem("bias_in"), sem("weights_in"), sem("late_in")
        half_in = [sem(f"half_in{i}") for i in range(2)]
        adj_in = [sem(f"adj_in{t}") for t in range(NT)]
        xT_in, x_in = sem("xT_in"), sem("x_in")
        q_stacked = [sem(f"q_stacked{h}") for h in range(HG)]
        k_stacked = [sem(f"k_stacked{h}") for h in range(HG)]
        x1_out = sem("x1_out")
        mask_made, deg_made, guard_step = sem("mask_made"), sem("deg_made"), sem("guard_step")
        half_made = sem("half_made")
        scored, lowered, probs_made = sem("scored"), sem("lowered"), sem("probs_made")
        turned_made = [sem(f"turned_made{j}") for j in range(2)]
        turned_kept = [sem(f"turned_kept{j}") for j in range(2)]
        pv_made, attn_made = sem("pv_made"), sem("attn_made")
        recip_made, cols_made, recipT_made, recipT_kept = sem("recip_made"), sem("cols_made"), sem("recipT_made"), sem("recipT_kept")
        qk_made, hi_made, lo_made = sem("qk_made"), sem("hi_made"), sem("lo_made")
        v_made, v_kept = sem("v_made"), sem("v_kept")
        dve_waited, sp_waited = sem("dve_waited"), sem("sp_waited")

        w_in, adjT_in, edges_made, deg_bias_made = sem("w_in"), [sem(f"adjT_in{t}") for t in range(6)], sem("edges_made"), sem("deg_bias_made")
        x1_in = [sem(f"x1_in{k}") for k in range(2)]
        out_sent = [sem(f"out_sent{k}") for k in range(2)]
        x1_biased, x1_turned, x1T_kept = sem("x1_biased"), sem("x1_turned"), sem("x1T_kept")
        mlp_made, msg_hi_made, msg_lo_made, own_made = sem("mlp_made"), sem("msg_hi_made"), sem("msg_lo_made"), sem("own_made")
        agg_made, half_added, agg_kept = sem("agg_made"), sem("half_added"), sem("agg_kept")
        stats2_made, moments2_made, eps2_made, rstd2_made, normed2 = sem("stats2_made"), sem("moments2_made"), sem("eps2_made"), sem("rstd2_made"), sem("normed2")
        wo_made, wo_kept, x_biased = sem("wo_made"), sem("wo_kept"), sem("x_biased")
        stats_made, moments_made, eps_made, rstd_made, normed = sem("stats_made"), sem("moments_made"), sem("eps_made"), sem("rstd_made"), sem("normed")

        def kept(kind, i, b, g):
            if kind == "r":
                return recipT_kept, pairs_before(b, g, i) + 1
            if kind == "wo":
                return wo_kept, (b - 1) * 4 + (i + 1)
            seg = b * G + (g + 1)
            return (lo_made, seg * 4 + (i + 1)) if i < 4 else (v_kept, seg * 2 + (i - 3))

        def segments(eng, segment):
            for g in range(G):
                segment(0, g, True, False, False)
            with eng.Fori(1, NB - 1) as b:
                for g in range(G):
                    segment(b, g, False, False, False)
            for g in range(G):
                segment(NB - 1, g, False, True, False)
            segment(NB, 0, False, False, True)

        def batches(eng, batch):
            for k in range(2):
                batch(k, k, k == 0, False)
            with eng.Fori(1, NB // 2 - 1) as pair:
                for k in range(2):
                    batch(pair * 2 + k, k, False, False)
            for k in range(2):
                batch(NB - 2 + k, k, False, k == 1)

        block = ctx.enter_context(nc.Block())

        @block.sync
        def _(sp):
            sp.sem_inc(x1_out, 16)
            def load_weight(w, w_dram, landed):
                sp.dma_start(w[:, :, :], w_dram.rearrange("(c p) n -> p c n", p=P)).then_inc(landed, 16)

            load_weight(wq_sb, wqT, wq_in)
            for i in range(2):
                cols = slice(i * HALF, (i + 1) * HALF)
                sp.dma_start(xT_sb[:, :, cols], xT[0][:, cols].rearrange("(c p) n -> p c n", p=P)).then_inc(half_in[i], 16)
            for b_sb, b_dram in ((bq_sb, bq), (bk_sb, bk)):
                sp.dma_start(b_sb[:, :], b_dram).then_inc(bias_in, 16)
            load_weight(wk_sb, wkT, wk_in)
            load_weight(wv_sb, wvT, weights_in)
            sp.dma_start(bv_sb[:, :], bv.rearrange("(a n) -> a n", a=1).broadcast_to([P, D])).then_inc(weights_in, 16)
            sp.dma_start(ident[:, :], ident_in).then_inc(weights_in, 16)

            def load_adj(t):
                if t >= 6:
                    sp.wait_ge(mask_made, t - 3)
                    sp.wait_ge(deg_made, t - 3)
                sp.dma_start(adj_sb[t], adj[t * P:(t + 1) * P, :]).then_inc(adj_in[t], 16)

            load_adj(0)
            load_adj(1)

            def stack(seg, g, free):
                sides = (((q_hi, q_lo, q_hi, q_lo), q_stack[g], q_stacked, 2), ((k_hi, k_hi, k_lo, k_lo), k_stack[g], k_stacked, 4))
                for h in range(HG):
                    for parts, dst, landed, i in sides:
                        if h == 0:
                            sp.wait_ge(lo_made, seg * 4 + i)
                            sp.sem_inc(sp_waited, 1)
                            if free is not None:
                                sp.wait_ge(scored, free)
                        for j, part in enumerate(parts):
                            if free is None and seg == 0 and j == h:
                                continue
                            sp.dma_start(dst[j * DH:(j + 1) * DH, h, :].bitcast(F32), part[h * DH:(h + 1) * DH, :].bitcast(F32)).then_inc(landed[h], 16)

            stack(0, 0, None)
            for t in range(2, NT):
                load_adj(t)
            load_weight(wo_sb, woT, late_in)
            for b_sb, b_dram in ((bo_sb, bo), (bias_sb, bias)):
                sp.dma_start(b_sb[:, :], b_dram.rearrange("(a n) -> a n", a=1).broadcast_to([P, D])).then_inc(late_in, 16)

            def segment(b, g, first, last, drain):
                def load_x():
                    if first:
                        sp.wait_ge(mask_made, 6)
                        sp.wait_ge(deg_made, 6)
                    else:
                        sp.wait_ge(wo_kept, b * 4)
                    sp.sem_inc(sp_waited, 1)
                    sp.dma_start(x_sb[:, :, :], x[b].rearrange("(t p) d -> p t d", p=P)).then_inc(x_in, 16)

                if g == 0 and not drain and not first:
                    load_x()
                if not (last and g == 1) and not drain:
                    stack(b * G + (g + 1), 1 - g, None if first and g == 0 else units_before(b, g, 0))
                if g == 0 and first:
                    load_x()
                if g == 0 and last:
                    sp.wait_ge(v_made, (b * G + 2) * 2)
                    sp.wait_ge(qk_made, (b * G + 2) * 4)
                    sp.dma_start(w_sb[:, :, :], wijT.rearrange("(c p) n -> p c n", p=P)).then_inc(w_in, 16)
                    for t in range(2):
                        sp.dma_start(edges_int[t], adjT[t * P:(t + 1) * P, :]).then_inc(adjT_in[t], 16)
                if g == 0 and not last and not drain:
                    sp.wait_ge(v_made, (b * G + 2) * 2)
                    sp.sem_inc(sp_waited, 1)
                    sp.wait_ge(qk_made, (b * G + 2) * 4)
                    sp.sem_inc(sp_waited, 1)
                    sp.dma_start(xT_sb[:, :, :], xT[b + 1].rearrange("(c p) n -> p c n", p=P)).then_inc(xT_in, 16)
                if g == 0 and not first and not drain:
                    sp.wait_ge(normed, b * NT)
                    sp.sem_inc(sp_waited, 1)
                    sp.dma_start(x1[b - 1].rearrange("(t p) d -> p t d", p=P), y_sb[:, :, :]).then_inc(x1_out, 16)

            segments(sp, segment)

            def load_edges(t, place):
                sp.dma_start(edges_int[place], adjT[t * P:(t + 1) * P, :]).then_inc(adjT_in[place], 16)

            sp.wait_ge(turned_made[1], NB * G * UNITS)
            sp.wait_ge(lowered, NB * G * UNITS)
            sp.dma_start(x1_sb[:, 0, :, :], x1[0].rearrange("(t p) d -> p t d", p=P)).then_inc(x1_in[0], 16)
            for t in range(2, 6):
                load_edges(t, t)
            def batch(b, k, first, last):
                if not last:
                    if not first:
                        sp.wait_ge(own_made, b * NT)
                        sp.sem_inc(sp_waited, 1)
                    sp.dma_start(x1_sb[:, 1 - k, :, :], x1[b + 1].rearrange("(t p) d -> p t d", p=P)).then_inc(x1_in[1 - k], 16)
                if not first:
                    sp.wait_ge(normed2, b * NT)
                    sp.sem_inc(sp_waited, 1)
                    sp.dma_start(out[b - 1].rearrange("(t p) d -> p t d", p=P), out_sb[1 - k][:, :, :]).then_inc(out_sent[1 - k], 16)
                if first:
                    for t in range(2):
                        sp.wait_ge(edges_made, t + 1)
                        load_edges(6 + t, t)
                    sp.wait_ge(normed, NB * NT)
                    sp.dma_start(x1[NB - 1].rearrange("(t p) d -> p t d", p=P), y_sb[:, :, :]).then_inc(x1_out, 16)
                if first:
                    sp.wait_ge(x1_out, (NB + 1) * 16)

            batches(sp, batch)
            for i in range(LAST_PARTS):
                tiles = slice(i * NT // LAST_PARTS, (i + 1) * NT // LAST_PARTS)
                sp.wait_ge(normed2, (NB - 1) * NT + tiles.stop)
                sp.dma_start(out[NB - 1].rearrange("(t p) d -> p t d", p=P)[:, tiles, :], out_sb[1][:, tiles, :]).then_inc(out_sent[1], 16)
            for k in range(2):
                sp.wait_ge(out_sent[k], (NB // 2 + (LAST_PARTS - 1 if k == 1 else 0)) * 16)

        @block.gpsimd
        def _(pool):
            pool.memset(neg_half[:, :], -0.5).then_inc(half_made, 1)
            pool.wait_ge(half_made, 1)
            pool.wait_ge(late_in, 3 * 16)

            def batch(b):
                pool.wait_ge(x_in, b * 16 + 16)
                pool.tensor_tensor(x_sb[:, :, :], x_sb[:, :, :], bo_sb[:, :].unsqueeze(1).broadcast_to([P, NT, D]),
                                   ALU.add).then_inc(x_biased, 1)
                pool.wait_ge(eps_made, b + 1)
                pool.tensor_tensor(rstd[:, :], var_eps[:, :], neg_half[:, :], ALU.pow).then_inc(rstd_made, 1)

            with pool.Fori(0, NB) as b:
                batch(b)

            def convolve(b, k, first, last):
                for t in range(NT):
                    pool.wait_ge(eps2_made, b * NT + (t + 1))
                    nc.gpsimd.tensor_tensor(rstd[:, t:t + 1], var_eps[:, t:t + 1], neg_half[:, t:t + 1], ALU.pow).then_inc(rstd2_made, 1)

            pool.wait_ge(normed, NB * NT)
            batches(pool, convolve)

        @block.scalar
        def _(act):
            act.wait_ge(bias_in, 2 * 16)

            def project(seg, g, i, reused):
                kind, half = PIECES[i]
                act.wait_ge(qk_made, seg * 4 + (i + 1))
                hi, bias, landed = (q_hi, bq_sb, q_stacked) if kind == "q" else (k_hi, bk_sb, k_stacked)
                bank = misc if reused else opening_banks[i]
                if reused and half == 0:
                    for h in range(HG):
                        act.wait_ge(landed[h], seg * (STACKS * 16))
                act.activation(hi[:, half * HALF:(half + 1) * HALF], bank[:, :], ACT.Identity, bias=bias[:, g:g + 1]).then_inc(hi_made, 1)

            def degree(t):
                act.wait_ge(adj_in[t], 16)
                if t > 0:
                    act.wait_ge(deg_made, t)
                act.activation(scratch[:, :], adj_sb[t], ACT.Copy, accum_out=deg[:, t:t + 1]).then_inc(deg_made, 1)

            for i in range(4):
                project(0, 0, i, False)

            def act_copy(dst, src):
                return nc.scalar.activation(dst, src, ACT.Copy)

            act.wait_ge(hi_made, 4)
            for kind, h in (("q", 0), ("k", 0), ("k", 1), ("q", 2)):
                keep_in_place(act_copy, h, kind)
            degree(0)
            degree(1)

            def segment(b, g, first, last, drain):
                pre_steps = {} if drain or (last and g == 1) else {u + 1: i for i, u in enumerate(PIECE_STEPS[g]) if i < 4}
                opening = first and g == 0
                for u in range(LAG + 5 if drain else UNITS):
                    t = u - LAG
                    if not (opening and t < 0) and not (drain and t >= 0):
                        act.wait_ge(turned_made[0], units_before(b, g, t) + 1)
                        if not (opening and t < PAIR):
                            act.wait_ge(pv_made, place_left(b, g, t))
                        nc.scalar.activation(turned_place(t, 0), turned[0][:, :].rearrange("p (k n) -> p k n", n=P), ACT.Copy).then_inc(turned_kept[0], 1)
                        if t % PAIR in ACT_BOTH:
                            act.wait_ge(turned_made[1], units_before(b, g, t) + 1)
                            nc.scalar.activation(turned_place(t, 1), turned[1][:, :].rearrange("p (k n) -> p k n", n=P), ACT.Copy).then_inc(turned_kept[1], 1)
                    p = (u - (RECIP_STEP + 2)) // PAIR
                    if (u - (RECIP_STEP + 2)) % PAIR == 0 and not (opening and p < 0) and not (drain and p >= 0):
                        act.wait_ge(recipT_made, pairs_before(b, g, p) + 1)
                        if not (opening and p < 1):
                            act.wait_ge(attn_made, pairs_before(b, g, p))
                        act.activation(recipT[:, :], misc[:, 0:2 * P], ACT.Copy).then_inc(recipT_kept, 1)
                    if u in pre_steps:
                        project(b * G + (g + 1), 1 - g, pre_steps[u], True)
                    if (u == 0 or not drain) and not (opening and u == 0):
                        e = u - 1
                        act.wait_ge(lowered, units_before(b, g, u))
                        act.activation(ring[:, e % RING, :], ring[:, e % RING, :], ACT.Exp, bias=low[:, e % RING:e % RING + 1],
                                       scale=-1.0, accum_out=sums[:, e // PAIR % 2, e % PAIR:e % PAIR + 1]).then_inc(probs_made, 1)
                    if opening and u % HG == 1 and u // HG + 2 < NT:
                        degree(u // HG + 2)

            segments(act, segment)

            def keep_turned(batch_no, i):
                act.wait_ge(x1_turned, batch_no * 4 + (i + 1))
                nc.scalar.activation(x1T[:, :, 2 * i * P:(2 * i + 2) * P], turned[i % 2][:, :].rearrange("p (c n) -> p c n", c=DC),
                                     ACT.Copy).then_inc(x1T_kept, 1)

            act.wait_ge(scored, NB * G * UNITS)
            for i in range(4):
                keep_turned(0, i)

            def batch(b, k, first, last):
                for t in range(NT):
                    act.wait_ge(mlp_made, b * NT + (t + 1))
                    if t == 0 and not first:
                        act.wait_ge(agg_made, b * NT)
                    nc.scalar.activation(msg[:, t, 0:D], mlp[:, t % 2, D:2 * D], ACT.Copy).then_inc(msg_hi_made, 1)
                    if first:
                        act.wait_ge(adjT_in[t % 6], t // 6 * 16 + 16)
                        nc.scalar.activation(edges[t], edges_int[t % 6], ACT.Copy).then_inc(edges_made, 1)
                if not last:
                    for i in range(4):
                        keep_turned(b + 1, i)

            batches(act, batch)

        @block.vector
        def _(dve):
            dve.wait_ge(bias_in, 2 * 16)

            def low_part(seg, g, i, reused):
                kind, half = PIECES[i]
                hi, lo, bias, landed = (q_hi, q_lo, bq_sb, q_stacked) if kind == "q" else (k_hi, k_lo, bk_sb, k_stacked)
                cols = slice(half * HALF, (half + 1) * HALF)
                bank = misc if reused else opening_banks[i]
                dve.wait_ge(hi_made, seg * 4 + (i + 1))
                if reused and half == 0:
                    for h in range(HG):
                        dve.wait_ge(landed[h], seg * (STACKS * 16))
                nc.vector.scalar_tensor_tensor(out=lo[:, cols], in0=bank[:, :], scalar=bias[:, g:g + 1], in1=hi[:, cols].bitcast(F32),
                                               op0=ALU.add, op1=ALU.subtract).then_inc(lo_made, 1)

            def keep_v(seg, g, i, free):
                dve.wait_ge(v_made, seg * 2 + (i + 1))
                if free is None and seg == 0:
                    dve.wait_ge(weights_in, 3 * 16)
                if free is not None:
                    dve.wait_ge(pv_made, free)
                bank = misc if free is not None else opening_banks[4 + i] if seg == 0 else second_v_banks[i]
                nc.vector.tensor_tensor(v_rows[g][:, 4 * i:4 * i + 4, :], bank[:, :].rearrange("p (t n) -> p t n", t=4),
                                        bv_sb[:, g * P:(g + 1) * P].unsqueeze(1).broadcast_to([P, 4, P]), ALU.add).then_inc(v_kept, 1)

            def make_mask(t):
                dve.wait_ge(adj_in[t], 16)
                nc.vector.tensor_scalar(mask[:, t, :], adj_sb[t], 0, MASKED, ALU.is_equal, ALU.mult).then_inc(mask_made, 1)

            def make_guard(t):
                row = slice(t, t + 1)
                dve.wait_ge(mask_made, t + 1)
                nc.vector.tensor_reduce(row_high[:, row], mask[:, t, :], AXX, ALU.max).then_inc(guard_step, 1)
                dve.wait_ge(guard_step, 4 * t + 1)
                nc.vector.tensor_scalar(has_edge[:, row], row_high[:, row], 0.0, None, ALU.is_equal).then_inc(guard_step, 1)
                dve.wait_ge(guard_step, 4 * t + 2)
                nc.vector.reciprocal(has_inv[:, row], has_edge[:, row]).then_inc(guard_step, 1)
                dve.wait_ge(guard_step, 4 * t + 3)
                nc.vector.tensor_tensor(guard[:, row], has_edge[:, row], has_inv[:, row], ALU.mult).then_inc(guard_step, 1)

            for i in range(4):
                low_part(0, 0, i, False)
            dve.wait_ge(lo_made, 4)
            for kind, h in (("q", 1), ("k", 2), ("q", 3), ("k", 3)):
                keep_in_place(nc.vector.tensor_copy, h, kind)
            for g in range(G):
                for i in range(2):
                    keep_v(g, g, i, None)
            make_mask(0)
            make_mask(1)

            def normalise(t):
                nc.vector.tensor_scalar(y_sb[:, t, :], y_sb[:, t, :], moments[:, t, 0:1], rstd[:, t:t + 1],
                                        ALU.subtract, ALU.mult).then_inc(normed, 1)

            def segment(b, g, first, last, drain):
                opening = first and g == 0
                pre = not drain and not (last and g == 1)
                pre_steps = {u + 1: i for i, u in enumerate(PIECE_STEPS[g]) if not (opening and i >= 4)} if pre else {}
                wo_steps = {u + 1: p for p, u in enumerate(WO_STEPS)} if g == 0 and not first else {}
                post = g == 0 and not first
                for u in range(DRAIN if drain else UNITS):
                    if post and STAT_STEP < u <= STAT_STEP + NT:
                        dve.wait_ge(stats_made, (b - 1) * NT + (u - STAT_STEP))
                    e = u - 1
                    if (u == 0 or not drain) and not (opening and u == 0):
                        dve.wait_ge(scored, units_before(b, g, e) + 1)
                        if not (opening and e < RING):
                            dve.wait_ge(turned_made[1], units_before(b, g, e) - (RING - 1))
                        if opening and e % HG == 0:
                            dve.wait_ge(mask_made, e // HG + 1)
                        dve.sem_inc(dve_waited, 1)
                        nc.vector.tensor_tensor_reduce(ring[:, e % RING, :], scores[:, e % 2, :], mask[:, e // HG % NT, :], -SCALE, 3e38,
                                                       ALU.add, ALU.min, low[:, e % RING:e % RING + 1]).then_inc(lowered, 1)
                    p = (u - ATTN_STEP) // PAIR
                    if (u - ATTN_STEP) % PAIR == 0 and not (opening and p < 0) and not (drain and p >= 0):
                        gp = g if p >= 0 else 1 - g
                        cols = slice(p % (NT // 2) * 2 * P, (p % (NT // 2) + 1) * 2 * P)
                        dve.wait_ge(pv_made, (pairs_before(b, g, p) + 1) * NT)
                        dve.wait_ge(recipT_kept, pairs_before(b, g, p) + 1)
                        if not first and p >= 0:
                            dve.wait_ge(wo_made, (b - 1) * 4 + (p + 1))
                        if opening and p == 0:
                            dve.wait_ge(deg_made, 2)
                        nc.vector.tensor_tensor(attnT[:, gp, cols], pv[:, 0:2 * P], recipT[:, :], ALU.mult).then_inc(attn_made, 1)
                    t = u - LAG
                    if t % PAIR not in ACT_BOTH and not (opening and t < 0) and not (drain and t >= 0):
                        dve.wait_ge(turned_made[1], units_before(b, g, t) + 1)
                        if not (opening and t < PAIR):
                            dve.wait_ge(pv_made, place_left(b, g, t))
                        nc.vector.tensor_copy(turned_place(t, 1), turned[1][:, :].rearrange("p (k n) -> p k n", n=P)).then_inc(turned_kept[1], 1)
                    if opening and u % HG == 1 and u // HG + 2 < NT:
                        make_mask(u // HG + 2)
                    if opening and u % HG == 2:
                        make_guard(u // HG)
                        if u // HG == NT - 1:
                            dve.wait_ge(guard_step, 4 * NT)
                    p = (u - RECIP_STEP) // PAIR
                    if (u - RECIP_STEP) % PAIR == 0 and not (opening and p < 0) and not (drain and p >= 0):
                        t = 2 * p % NT
                        dve.wait_ge(probs_made, units_before(b, g, PAIR * p + PAIR))
                        nc.vector.reciprocal(recip[:, :], sums[:, p % 2, :]).then_inc(recip_made, 1)
                        dve.wait_ge(recip_made, pairs_before(b, g, p) + 1)
                        if not (opening and p < 1):
                            dve.wait_ge(recipT_made, pairs_before(b, g, p))
                        if opening:
                            dve.wait_ge(guard_step, 4 * t + 8)
                        nc.vector.tensor_tensor(recip_cols[:, :, :].rearrange("p (t h) d -> p t h d", t=2),
                                                recip[:, :].rearrange("p (t h) -> p t h", t=2).unsqueeze(3).broadcast_to([P, 2, HG, DH]),
                                                guard[:, t:t + 2].unsqueeze(2).unsqueeze(3).broadcast_to([P, 2, HG, DH]), ALU.mult).then_inc(cols_made, 1)
                    if u in pre_steps:
                        i = pre_steps[u]
                        if i < 4:
                            low_part(b * G + (g + 1), 1 - g, i, True)
                        else:
                            keep_v(b * G + (g + 1), 1 - g, i - 4, pairs_before(b, g, 0) * NT)
                    if u in wo_steps:
                        p = wo_steps[u]
                        dve.wait_ge(wo_made, (b - 1) * 4 + (p + 1))
                        if p == 0:
                            dve.wait_ge(x_biased, b)
                            dve.wait_ge(x1_out, b * 16)
                        nc.vector.tensor_tensor(y_sb[:, 2 * p:2 * p + 2, :], misc[:, :].rearrange("p (t n) -> p t n", t=2),
                                                x_sb[:, 2 * p:2 * p + 2, :], ALU.add).then_inc(wo_kept, 1)
                    if post and STAT_STEP <= u < STAT_STEP + NT:
                        t = u - STAT_STEP
                        dve.wait_ge(wo_kept, (b - 1) * 4 + (t // 2 + 1))
                        nc.vector.bn_stats(stats[:, t, :], y_sb[:, t, :]).then_inc(stats_made, 1)
                    if post and STAT_STEP < u <= STAT_STEP + NT:
                        t = u - STAT_STEP - 1
                        nc.vector.bn_aggr(moments[:, t, :], stats[:, t, :]).then_inc(moments_made, 1)
                    if post and u == EPS_STEP:
                        dve.wait_ge(moments_made, b * NT)
                        nc.vector.tensor_scalar(var_eps[:, :], moments[:, :, 1], EPS, None, ALU.add).then_inc(eps_made, 1)
                    if post and not drain and NORM_STEP <= u < NORM_STEP + NT:
                        dve.wait_ge(rstd_made, b)
                        normalise(u - NORM_STEP)

            segments(dve, segment)

            dve.wait_ge(late_in, 3 * 16)
            dve.wait_ge(wo_kept, NB * 4)
            dve.wait_ge(rstd_made, NB)
            dve.wait_ge(pv_made, pairs_before(NB, 0, 0) * NT)

            def norm(b, k, t):
                dve.wait_ge(rstd2_made, b * NT + (t + 1))
                nc.vector.tensor_scalar(out_sb[k][:, t, :], out_sb[k][:, t, :], moments[:, t, 0:1], rstd[:, t:t + 1],
                                        ALU.subtract, ALU.mult).then_inc(normed2, 1)

            def moments_of(b, t):
                nc.vector.bn_aggr(moments[:, t, :], stats[:, t, :]).then_inc(moments2_made, 1)

            def eps_of(b, t):
                dve.wait_ge(moments2_made, b * NT + (t + 1))
                nc.vector.tensor_scalar(var_eps[:, t:t + 1], moments[:, t, 1:2], EPS, None, ALU.add).then_inc(eps2_made, 1)

            def batch(b, k, first, last):
                dve.wait_ge(x1_in[k], (b - k) * 8 + 16)
                for t in range(NT):
                    if first:
                        nc.vector.tensor_scalar(deg_bias[:, t, :], bias_sb[:, :], deg[:, t:t + 1], None, ALU.mult).then_inc(deg_bias_made, 1)
                        dve.wait_ge(deg_bias_made, t + 1)
                    nc.vector.tensor_tensor(x1_bias[:, t, :], x1_sb[:, k, t, :], deg_bias[:, t, :], ALU.add).then_inc(x1_biased, 1)
                    dve.wait_ge(msg_hi_made, b * NT + (t + 1))
                    nc.vector.tensor_tensor(msg[:, t, D:2 * D], mlp[:, t % 2, D:2 * D], msg[:, t, 0:D].bitcast(F32),
                                            ALU.subtract).then_inc(msg_lo_made, 1)
                    dve.wait_ge(x1_biased, b * NT + (t + 1))
                    nc.vector.scalar_tensor_tensor(out=own[:, t, :], in0=mlp[:, t % 2, 0:D], scalar=deg[:, t:t + 1],
                                                   in1=x1_bias[:, t, :], op0=ALU.mult, op1=ALU.add).then_inc(own_made, 1)
                    if first:
                        normalise(t)
                    elif t < 3:
                        norm(b - 1, 1 - k, NT - 3 + t)

                dve.wait_ge(own_made, b * NT + NT)
                if not (isinstance(b, int) and b < 2):
                    dve.wait_ge(out_sent[k], (b - k) * 8)
                for t in range(NT):
                    done = b * NT + (t + 1)
                    dve.wait_ge(agg_made, done)
                    nc.vector.tensor_tensor(out_sb[k][:, t, :], agg[:, t % 2, 0:D], own[:, t, :], ALU.add).then_inc(half_added, 1)
                    if t >= 3:
                        norm(b, k, t - 3)
                    if t > 0:
                        dve.wait_ge(stats2_made, done - 1)
                    dve.wait_ge(half_added, done)
                    nc.vector.tensor_tensor(out_sb[k][:, t, :], agg[:, t % 2, D:2 * D], out_sb[k][:, t, :], ALU.add).then_inc(agg_kept, 1)
                    if t > 0:
                        moments_of(b, t - 1)
                    dve.wait_ge(agg_kept, done)
                    nc.vector.bn_stats(stats[:, t, :], out_sb[k][:, t, :]).then_inc(stats2_made, 1)
                    if t > 0:
                        eps_of(b, t - 1)
                dve.wait_ge(stats2_made, b * NT + NT)
                dve.sem_inc(dve_waited, 1)
                moments_of(b, NT - 1)
                eps_of(b, NT - 1)

            batches(dve, batch)
            for t in range(NT - 3, NT):
                norm(NB - 1, 1, t)

        @block.tensor
        def _(pe):
            pe.wait_ge(wq_in, 16)

            def project(seg, g, i, dst):
                kind, half = PIECES[i]
                if kind == "v":
                    for t in range(4):
                        rows = slice((4 * half + t) * P, (4 * half + t + 1) * P)
                        for c in range(DC):
                            last = nc.tensor.matmul(dst[:, t * P:(t + 1) * P], xT_sb[:, c, rows], wv_sb[:, c, g * P:(g + 1) * P],
                                                    start=(c == 0), stop=(c == DC - 1))
                    last.then_inc(v_made, 1)
                else:
                    w = wq_sb if kind == "q" else wk_sb
                    for c in range(DC):
                        last = nc.tensor.matmul(dst[:, :], w[:, c, g * P:(g + 1) * P], xT_sb[:, c, half * HALF:(half + 1) * HALF],
                                                start=(c == 0), stop=(c == DC - 1))
                    last.then_inc(qk_made, 1)

            for i in range(len(PIECES)):
                if i < 2:
                    pe.wait_ge(half_in[i], 16)
                if i == 2:
                    pe.wait_ge(wk_in, 16)
                if i == 4:
                    pe.wait_ge(weights_in, 3 * 16)
                project(0, 0, i, opening_banks[i])
            for i in range(2):
                project(1, 1, 4 + i, second_v_banks[i])
            pe.wait_ge(lo_made, 4)
            pe.wait_ge(v_kept, 2 * G)

            def multiply(b, g, u, opening, drain, part):
                p, k = (u - PV_STEP) // PAIR, (u - PV_STEP) % PAIR
                if part == (FIRST_KEY_PART if k == 0 else 0) and not (opening and p < 0) and not (drain and p >= 0):
                    gp = g if p >= 0 else 1 - g
                    if k == 0:
                        for j in range(2):
                            pe.wait_ge(turned_kept[j], units_before(b, g, PAIR * (p + 1)))
                        if not (opening and p < 1):
                            pe.wait_ge(attn_made, pairs_before(b, g, p))
                        if p == 0:
                            pe.wait_ge(v_kept, (b * G + (g + 1)) * 2)
                    for h in range(HG):
                        mm = nc.tensor.matmul(pv[h * DH:(h + 1) * DH, 0:2 * P], v_rows[gp][:, k, h * DH:(h + 1) * DH],
                                              turned_of(p, h, k), start=(k == 0), stop=(k == NT - 1))
                    mm.then_inc(pv_made, 1)

            def segment(b, g, first, last, drain):
                opening = first and g == 0
                users = misc_users(g, first, last, drain)
                for u in range(WO_STEPS[-1] + 1 if drain else UNITS):
                    multiply(b, g, u, opening, drain, 0)
                    t = u - LAG
                    turn = not (opening and t < 0) and not (drain and t >= 0)
                    for j in range(2):
                        if turn:
                            if j == 0:
                                pe.wait_ge(probs_made, units_before(b, g, t) + 1)
                            if not (opening and t < 1):
                                pe.wait_ge(turned_kept[j], units_before(b, g, t))
                            for c in range(4):
                                k = 4 * j + c
                                mm = nc.tensor.transpose(turned[j][:, c * P:(c + 1) * P], ring[:, t % RING, k * P:(k + 1) * P], ident[:, :])
                            mm.then_inc(turned_made[j], 1)
                        if not drain:
                            if j == 0:
                                if not (opening and u < 2):
                                    pe.wait_ge(lowered, units_before(b, g, u) - 1)
                                if u < HG:
                                    pe.wait_ge(q_stacked[u], (b * G + (g + 1)) * (STACKS * 16))
                                    pe.wait_ge(k_stacked[u], (b * G + (g + 1)) * (STACKS * 16))
                            h, q = u % HG, u // HG
                            mm = nc.tensor.matmul(scores[:, u % 2, j * HALF:(j + 1) * HALF], q_stack[g][:, h, q * P:(q + 1) * P],
                                                  k_stack[g][:, h, j * HALF:(j + 1) * HALF], start=True, stop=True)
                            if j == 1:
                                mm.then_inc(scored, 1)
                        multiply(b, g, u, opening, drain, j + 1)
                    for n, (at, kind, i) in enumerate(users):
                        if at != u:
                            continue
                        if n > 0:
                            pe.wait_ge(*kept(*users[n - 1][1:], b, g))
                        elif not opening:
                            before = misc_users(1 - g, first, last and g == 1 or drain, False)[-1]
                            pe.wait_ge(*kept(*before[1:], *((b, 0) if g == 1 else (b - 1, 1))))
                        if kind == "r":
                            pe.wait_ge(cols_made, pairs_before(b, g, i) + 1)
                            for j in range(2):
                                mm = nc.tensor.transpose(misc[:, j * P:(j + 1) * P],
                                                         recip_cols[:, j * HG:(j + 1) * HG, :].rearrange("p h d -> p (h d)"), ident[:, :])
                            mm.then_inc(recipT_made, 1)
                        elif kind == "wo":
                            pe.wait_ge(late_in, 3 * 16)
                            pe.wait_ge(attn_made, pairs_before(b - 1, 1, i + 1))
                            for j in range(2):
                                rows = slice((2 * i + j) * P, (2 * i + j + 1) * P)
                                for c in range(G):
                                    mm = nc.tensor.matmul(misc[:, j * D:(j + 1) * D], attnT[:, c, rows], wo_sb[:, c, :],
                                                          start=(c == 0), stop=(c == G - 1))
                            mm.then_inc(wo_made, 1)
                        else:
                            if g == 1 and i == 0:
                                pe.wait_ge(xT_in, b * 16 + 16)
                            project(b * G + (g + 1), 1 - g, i, misc)

            segments(pe, segment)

            def turn(batch_no, k, i, opening):
                if i == 0:
                    pe.wait_ge(x1_in[k], (batch_no - k) * 8 + 16)
                if not (opening and i < 2):
                    pe.wait_ge(x1T_kept, batch_no * 4 + (i - 1))
                for j in range(2):
                    for c in range(DC):
                        mm = nc.tensor.transpose(turned[i % 2][:, c * D + j * P:c * D + (j + 1) * P],
                                                 x1_sb[:, k, 2 * i + j, c * P:(c + 1) * P], ident[:, :])
                mm.then_inc(x1_turned, 1)

            for j in range(2):
                pe.wait_ge(turned_kept[j], NB * G * UNITS)
            for i in range(4):
                turn(0, 0, i, True)
            pe.wait_ge(w_in, 16)
            pe.wait_ge(lowered, NB * G * UNITS)

            def batch(b, k, first, last):
                for t in range(NT):
                    if t % 2 == 0:
                        pe.wait_ge(x1T_kept, b * 4 + (t // 2 + 1))
                    if t >= 2:
                        pe.wait_ge(own_made, b * NT + (t - 1))
                    elif not first:
                        pe.wait_ge(own_made, b * NT)
                    for c in range(DC):
                        mm = nc.tensor.matmul(mlp[:, t % 2, :], x1T[:, c, t * P:(t + 1) * P], w_sb[:, c, :],
                                              start=(c == 0), stop=(c == DC - 1))
                    mm.then_inc(mlp_made, 1)
                if not last:
                    turn(b + 1, 1 - k, 0, False)
                    turn(b + 1, 1 - k, 1, False)
                if first:
                    pe.wait_ge(edges_made, NT)
                pe.wait_ge(msg_lo_made, b * NT + NT)
                for t in range(NT):
                    if t >= 2:
                        pe.wait_ge(agg_kept, b * NT + (t - 1))
                    elif not first:
                        pe.wait_ge(agg_kept, b * NT)
                    for j in range(NT):
                        mm = nc.tensor.matmul(agg[:, t % 2, :], edges[j][:, t * P:(t + 1) * P], msg[:, j, :],
                                              start=(j == 0), stop=(j == NT - 1))
                    mm.then_inc(agg_made, 1)
                    if t in (1, 3) and not last:
                        turn(b + 1, 1 - k, (t + 3) // 2, False)

            batches(pe, batch)


def kernel(x, adj, L0_gnn_Wq, L0_gnn_bq, L0_gnn_Wk, L0_gnn_bk, L0_gnn_Wv, L0_gnn_bv, L0_gnn_Wo, L0_gnn_bo, L1_gnn_W, L1_gnn_b):
    import numpy as np
    import concourse.bacc as bacc
    from concourse.bass_utils import run_bass_kernel_spmd

    def laid(a):
        return np.ascontiguousarray(a)

    x, adj, w1 = np.asarray(x), np.asarray(adj), np.asarray(L1_gnn_W)
    arrays = {
        "x": laid(x), "xT": laid(x.transpose(0, 2, 1)), "adj": laid(adj), "adjT": laid(adj.T),
        "ident": np.eye(P, dtype=np.float32),
        "wqT": laid(np.asarray(L0_gnn_Wq).T), "bq": laid(np.asarray(L0_gnn_bq).reshape(G, P).T), "wkT": laid(np.asarray(L0_gnn_Wk).T), "bk": laid(np.asarray(L0_gnn_bk).reshape(G, P).T),
        "wvT": laid(np.asarray(L0_gnn_Wv).T), "bv": laid(L0_gnn_bv), "woT": laid(np.asarray(L0_gnn_Wo).T), "bo": laid(L0_gnn_bo),
        "wijT": laid(w1.reshape(D, 2, D).transpose(2, 1, 0).reshape(D, 2 * D)), "bias": laid(L1_gnn_b),
    }
    nc = bacc.Bacc("TRN2", target_bir_lowering=False, num_devices=1)
    args = [nc.dram_tensor(n + "_dram", a.shape, mybir.dt.from_np(a.dtype), kind="ExternalInput").ap() for n, a in arrays.items()]
    out = nc.dram_tensor("out_dram", x.shape, F32, kind="ExternalOutput").ap()
    x1 = nc.dram_tensor("x1_dram", x.shape, F32, kind="Internal").ap()
    gnn_layers(nc, *args, x1, out)
    r = run_bass_kernel_spmd(nc, [{n + "_dram": a for n, a in arrays.items()}], core_ids=[0])
    return r.results[0]["out_dram"]
```
